# Optimizing a Trainium2 kernel written in Bass

```python
import numpy as np
import jax
import jax.numpy as jnp

def _softmax(x, axis=-1):
    return jax.nn.softmax(x, axis=axis)

def _gelu(x):
    return jax.nn.gelu(x, approximate=True)

def _silu(x):
    return jax.nn.silu(x)

def _sigmoid(x):
    return jax.nn.sigmoid(x)

def _layernorm(x, axis=-1, eps=1e-05):
    m = jnp.mean(x, axis=axis, keepdims=True)
    v = jnp.var(x, axis=axis, keepdims=True)
    return (x - m) / jnp.sqrt(v + eps)

def _scatter_add(tgt, idx, src, axis=0):
    return tgt.at[idx].add(src)

def _segment_sum(src, seg, n):
    return jax.ops.segment_sum(src, seg, n)
kernel_name = 'mk_adj_resnorm_d2_adj_r2_dcb7cd'

def setup_inputs(seed: int=0):
    np.random.seed(seed)
    _w = jnp.asarray

    def _rec_inputs():
        import jax
        import jax.numpy as jnp
        _gk = jax.random.key(seed)
        x = 7.22e-05 + 1 * jax.random.normal(jax.random.fold_in(_gk, 1), (64, 128, 256), jnp.float32)
        _w = (1.0 + jnp.arange(128, dtype=jnp.float32)) ** (-0.5)
        _w = _w / _w.mean()
        _pij = jnp.clip(0.0625 * _w[:, None] * _w[None, :], 0.0, 1.0)
        _a = jax.random.uniform(jax.random.fold_in(_gk, 2), (64, 128, 128)) < _pij
        _a = jnp.logical_or(_a, jnp.eye(128, dtype=bool))
        _af = _a.astype(jnp.float32)
        _af = _af * jax.random.uniform(jax.random.fold_in(_gk, 3), (64, 128, 128), jnp.float32, 0.05, 1)
        adj = _af
        _nm = jnp.ones((64, 128), dtype=bool)
        nodemask = jnp.where(_nm, 1.0, 0.0).astype(jnp.float32)
        return (x, adj, nodemask)
    x, adj, nodemask = _rec_inputs()

    def _L0_gnn_setup():
        import jax, jax.numpy as jnp
        import numpy as np
        B, N, IN_DIM, ATT_DIM = (2, 4096, 256, 256)
        key = jax.random.key(seed)
        k1, k2, k3, k4 = jax.random.split(key, 4)
        X = jax.random.normal(k1, (B, N, IN_DIM), dtype=jnp.float32)
        adj = jax.random.uniform(k2, (B, N, N), dtype=jnp.float32)
        mask = jnp.ones((B, N), dtype=jnp.float32)
        Wqk = jax.random.normal(k3, (IN_DIM, 2 * ATT_DIM), dtype=jnp.float32) / np.sqrt(IN_DIM)
        Wv = jax.random.normal(k4, (IN_DIM, IN_DIM), dtype=jnp.float32) / np.sqrt(IN_DIM)
        return {'X': X, 'adj': adj, 'mask': mask, 'Wqk': Wqk, 'Wv': Wv}
    _L0_gnn_all = _L0_gnn_setup()
    _L0_gnn_in = {k: v for k, v in _L0_gnn_all.items() if k in ('Wqk', 'Wv')}
    del _L0_gnn_all

    def _L1_gnn_setup():
        import jax, jax.numpy as jnp
        import numpy as np
        EPS_LN = 1e-05

        def hypergraph_conv(x, adj, W, b):
            N, C, _ = adj.shape
            H = (adj != 0).astype(x.dtype)
            w = adj.reshape(N, -1)[:, :C]
            xw = jnp.einsum('ncd,hd->nch', x, W)
            Dn = jnp.einsum('nce,ne->nc', H, w)
            Dn = jnp.where(Dn > 0, 1.0 / Dn, 0.0)
            Be = H.sum(axis=1)
            Be = jnp.where(Be > 0, 1.0 / Be, 0.0)
            m = Be[:, :, None] * jnp.einsum('nce,nch->neh', H, xw)
            out = Dn[:, :, None] * jnp.einsum('nce,neh->nch', H, m)
            return out + b

        def layer_norm(x, g, b):
            mu = jnp.mean(x, axis=-1, keepdims=True)
            var = jnp.var(x, axis=-1, keepdims=True)
            return (x - mu) * jax.lax.rsqrt(var + EPS_LN) * g + b
        key = jax.random.key(seed)
        ks = jax.random.split(key, 4)
        N, C, Din, Dh, Dout = (16, 512, 256, 512, 256)
        x = jax.random.normal(ks[0], (N, C, Din), dtype=jnp.float32)
        adj = jax.random.uniform(ks[1], (N, C, C), dtype=jnp.float32, minval=0.1, maxval=1.0)
        W1 = jax.random.normal(ks[2], (Dh, Din), dtype=jnp.float32) * (1.0 / np.sqrt(Din))
        b1 = jnp.zeros((Dh,), dtype=jnp.float32)
        gamma = jnp.ones((Dh,), dtype=jnp.float32)
        beta = jnp.zeros((Dh,), dtype=jnp.float32)
        W2 = jax.random.normal(ks[3], (Dout, Dh), dtype=jnp.float32) * (1.0 / np.sqrt(Dh))
        b2 = jnp.zeros((Dout,), dtype=jnp.float32)
        return {'x': x, 'adj': adj, 'W1': W1, 'b1': b1, 'gamma': gamma, 'beta': beta, 'W2': W2, 'b2': b2}
    _L1_gnn_all = _L1_gnn_setup()
    _L1_gnn_in = {k: v for k, v in _L1_gnn_all.items() if k in ('W1', 'b1', 'gamma', 'beta', 'W2', 'b2')}
    del _L1_gnn_all
    return {'x': x, 'adj': adj, 'nodemask': nodemask, 'L0_gnn_Wqk': _L0_gnn_in['Wqk'], 'L0_gnn_Wv': _L0_gnn_in['Wv'], 'L1_gnn_W1': _L1_gnn_in['W1'], 'L1_gnn_b1': _L1_gnn_in['b1'], 'L1_gnn_gamma': _L1_gnn_in['gamma'], 'L1_gnn_beta': _L1_gnn_in['beta'], 'L1_gnn_W2': _L1_gnn_in['W2'], 'L1_gnn_b2': _L1_gnn_in['b2']}

def reference(x, adj, nodemask, L0_gnn_Wqk, L0_gnn_Wv, L1_gnn_W1, L1_gnn_b1, L1_gnn_gamma, L1_gnn_beta, L1_gnn_W2, L1_gnn_b2):
    import jax
    import jax.numpy as jnp

    def _L0_gnn_ref(X, adj, mask, Wqk, Wv):
        import jax, jax.numpy as jnp
        import numpy as np
        B, N, IN_DIM, ATT_DIM = (2, 4096, 256, 256)
        qk = X @ Wqk
        q, k = jnp.split(qk, 2, axis=-1)
        v = X @ Wv
        att_dim = q.shape[-1]
        inv_scale = 1.0 / jnp.sqrt(jnp.float32(att_dim))
        k_m = k * mask[:, :, None]
        agg = jnp.einsum('bij,bjd->bid', adj, k_m)
        w = inv_scale * mask * jnp.einsum('bid,bid->bi', q, agg)
        L = jax.nn.softmax(w, axis=1)[:, :, None] * v
        return L

    def _L1_gnn_ref(x, adj, W1, b1, gamma, beta, W2, b2):
        import jax, jax.numpy as jnp
        import numpy as np
        EPS_LN = 1e-05

        def hypergraph_conv(x, adj, W, b):
            N, C, _ = adj.shape
            H = (adj != 0).astype(x.dtype)
            w = adj.reshape(N, -1)[:, :C]
            xw = jnp.einsum('ncd,hd->nch', x, W)
            Dn = jnp.einsum('nce,ne->nc', H, w)
            Dn = jnp.where(Dn > 0, 1.0 / Dn, 0.0)
            Be = H.sum(axis=1)
            Be = jnp.where(Be > 0, 1.0 / Be, 0.0)
            m = Be[:, :, None] * jnp.einsum('nce,nch->neh', H, xw)
            out = Dn[:, :, None] * jnp.einsum('nce,neh->nch', H, m)
            return out + b

        def layer_norm(x, g, b):
            mu = jnp.mean(x, axis=-1, keepdims=True)
            var = jnp.var(x, axis=-1, keepdims=True)
            return (x - mu) * jax.lax.rsqrt(var + EPS_LN) * g + b
        h = jax.nn.relu(hypergraph_conv(x, adj, W1, b1))
        h = layer_norm(h, gamma, beta)
        y = hypergraph_conv(h, adj, W2, b2)
        return y + x
    x = _layernorm(x + _L0_gnn_ref(x, adj, nodemask, L0_gnn_Wqk, L0_gnn_Wv), axis=-1)
    x = _layernorm(x + _L1_gnn_ref(x, adj, L1_gnn_W1, L1_gnn_b1, L1_gnn_gamma, L1_gnn_beta, L1_gnn_W2, L1_gnn_b2), axis=-1)
    return x

_drawn_inputs = setup_inputs


def setup_inputs(seed=0):
    import zlib

    import numpy as np

    out = dict(_drawn_inputs(seed))
    spreads = {'L1_gnn_b1': (0.0, 0.1),
     'L1_gnn_gamma': (1.0, 0.2),
     'L1_gnn_beta': (0.0, 0.1),
     'L1_gnn_b2': (0.0, 0.1)}
    factors = {}
    for name, (base, spread) in spreads.items():
        noise = np.random.default_rng([zlib.crc32(name.encode()), seed]).standard_normal(out[name].shape)
        drawn = base * np.exp(spread * noise) if base else spread * noise
        out[name] = jnp.asarray(drawn.astype(out[name].dtype))
    for name, factor in factors.items():
        out[name] = (out[name] * factor).astype(out[name].dtype)
    return out
```

```python
from contextlib import ExitStack

import concourse.bass as bass
from concourse import mybir

ALU = mybir.AluOpType
ACT = mybir.ActivationFunctionType
F32 = mybir.dt.float32
F32R = mybir.dt.float32r
AX_X = mybir.AxisListType.X
P = 128
EPS = 1e-5


class Group:

    def __init__(self, it, k):
        self.n = it * 2 + k
        self.half = it + k // 2
        self.par = k % 2


def wait(eng, sem, value):
    if isinstance(value, int) and value <= 0:
        return
    eng.wait_ge(sem, value)


def plain(eng, sem):
    eng.wait_ge(sem, 1)


def build_program(nc, x, adj, nodemask, Wqk, Wv, W1, b1, gamma, beta, W2, b2, out):
    B, N, D = x.shape
    DH = W1.shape[0]
    GR = 4
    NG = B // GR
    DC = D // P
    HC = DH // P
    GN = GR * N
    W2N = D + 2
    assert N == P and DC == 2 and HC == 4 and GN == 512 and NG % 2 == 0

    with ExitStack() as ctx:
        def sb(name, shape, dt=F32):
            return ctx.enter_context(nc.sbuf_tensor(name, shape, dt))

        def sem(name):
            return ctx.enter_context(nc.semaphore(name))

        ident = sb("ident", [P, P])
        neg_half = sb("neg_half", [P, GR])
        ones_mean = sb("ones_mean", [P, P])
        b2_rows = sb("b2_rows", [P, D])
        cbeta = sb("cbeta", [P, D])
        vec_rows = sb("vec_rows", [3 * HC, P])
        vec_cols = sb("vec_cols", [P, 3 * HC])
        m_hi, m_lo = sb("m_hi", [P, DC, D], F32R), sb("m_lo", [P, DC, D], F32R)
        wv_hi, wv_lo = sb("wv_hi", [P, DC, D], F32R), sb("wv_lo", [P, DC, D], F32R)
        w1_hi, w1_lo = sb("w1_hi", [P, DC, DH], F32R), sb("w1_lo", [P, DC, DH], F32R)
        w2_hi, w2_lo = sb("w2_hi", [P, HC, W2N], F32R), sb("w2_lo", [P, HC, W2N], F32R)

        x_in = sb("x_in", [P, 2, GR, D])
        a_in = sb("a_in", [P, 2, GR, N])
        mask_in = sb("mask_in", [P, 2, GR, N])
        edge_in = sb("edge_in", [P, 2, GR, N])
        mrow_in = sb("mrow_in", [GR, 2, N])
        xt = sb("xt", [P, DC, GN])
        xt_hi, xt_lo = sb("xt_hi", [P, DC, GN], F32R), sb("xt_lo", [P, DC, GN], F32R)
        tt = sb("tt", [P, DC, GN])
        am = sb("am", [P, GR, N])
        dot_junk = sb("dot_junk", [P, GR, N])
        w_col = sb("w_col", [P, GR])
        w_row = sb("w_row", [GR, N])
        w_max = sb("w_max", [GR, 1])
        w_bias = sb("w_bias", [GR, 1])
        e_row = sb("e_row", [GR, N])
        e_sum = sb("e_sum", [GR, 1])
        e_inv = sb("e_inv", [GR, 1])
        p_row = sb("p_row", [GR, N])
        p_col = sb("p_col", [P, GR])
        hn = sb("hn", [P, GR, N])
        ht = sb("ht", [P, GR, N])
        he = sb("he", [P, GR, N])
        pn = sb("pn", [P, GR, N])
        rr = sb("rr", [P, GR, N])
        cnt = sb("cnt", [P, GR])
        cnt1 = sb("cnt1", [P, GR])
        be = sb("be", [P, GR])
        deg = sb("deg", [P, GR])
        deg1 = sb("deg1", [P, GR])
        deg_inv = sb("deg_inv", [P, GR])
        dn = sb("dn", [P, GR])
        gp = sb("gp", [P, 2, GR, N])
        r1 = sb("r1", [P, GR, D])
        st1 = sb("st1", [P, GR, 6])
        mv1 = sb("mv1", [P, GR, 2])
        ve1 = sb("ve1", [P, GR])
        rstd1 = sb("rstd1", [P, GR])
        x1 = sb("x1", [P, 2, GR, D])
        zt_hi, zt_lo = sb("zt_hi", [P, DC, GN], F32R), sb("zt_lo", [P, DC, GN], F32R)
        h = sb("h", [P, HC, GN])
        h_hi, h_lo = sb("h_hi", [P, HC, GN], F32R), sb("h_lo", [P, HC, GN], F32R)
        sq = sb("sq", [P, HC, GN])
        q1 = sb("q1", [P, 2, GN])
        q = sb("q", [P, GN])
        ssq = sb("ssq", [P, GR])
        hmu2 = sb("hmu2", [P, GR])
        hvar = sb("hvar", [P, GR])
        hve = sb("hve", [P, GR])
        rs = sb("rs", [P, GR])
        u0 = sb("u0", [P, GR, W2N])
        u = sb("u", [P, GR, D])
        base0 = sb("base0", [P, GR, D])
        base = sb("base", [P, GR, D])
        f = sb("f", [P, GR, D])
        st2 = sb("st2", [P, GR, 6])
        mv2 = sb("mv2", [P, GR, 2])
        ve2 = sb("ve2", [P, GR])
        rstd2 = sb("rstd2", [P, GR])
        nmr = sb("nmr", [P, GR])
        y = sb("y", [P, 2, GR, D])

        wqk_raw = sb("wqk_raw", [P, DC, 2 * D])
        wv_raw = sb("wv_raw", [P, DC, D])
        w1_raw = sb("w1_raw", [P, HC, D])
        w2_raw = sb("w2_raw", [P, DC, DH])
        wq_t = h[:, 0, :].rearrange("p (a d) -> p a d", a=DC)
        wk_t = h[:, 1, :].rearrange("p (a d) -> p a d", a=DC)
        w2_t = sq[:, 0:2, :].rearrange("p a (b d) -> p (a b) d", d=D)
        w2_g = sq[:, 2:4, :].rearrange("p a (b d) -> p (a b) d", d=D)
        w2_c = h[:, 2:4, :].rearrange("p a (b d) -> p (a b) d", d=D)
        beta_rows = xt[:, 0, :].rearrange("p (a d) -> p a d", a=HC)

        ps = ctx.enter_context(nc.psum_tensor("ps", [P, 8, 512], F32))
        X_T, A_T, SMALL = (0, 2), 3, 2
        ps_xt = ps[:, 0:2, :]
        ps_v = ps[:, 0:2, :].rearrange("p a (b d) -> p (a b) d", d=D)
        ps_s = ps[:, 2, :].rearrange("p (g n) -> p g n", g=GR)
        ps_at = ps[:, 3, :].rearrange("p (g n) -> p g n", g=GR)
        ps_zt = ps[:, 4:6, :]
        W_BANK = (4, 5, 6, 7)
        ps_c2 = ps[:, 6:8, :].rearrange("p a (b d) -> p (a b) d", d=D)

        s = {name: sem(name) for name in """
            w_loaded ident_zero ident_ready consts_ready setup_tr setup_copied m_done m_hi_ready m_lo_ready
            vec_ready w2g_ready cb_done w2c_ready setup_act setup_dve
            xt_done at_done t_done s_done pt_done v_done wt_done pcol_done g_done z_done w1_done w2_done qt_done c2_done
            xt_ready xt_hi_ready xt_lo_ready tt_ready am_ready w_ready wrow_ready wmax_ready wbias_ready e_ready
            einv_ready prow_ready pcol_ready
            hn_ready ht_ready cnt_ready cnt1_ready be_ready he_ready deg_ready deg1_ready dinv_ready dn_ready pn_ready
            rr_ready gp_ready r1_ready st1_ready mv1_ready ve1_ready rstd1_ready x1_ready
            zt_hi_ready zt_lo_ready h_ready h_hi_ready h_lo_ready sq_ready q1_ready q_ready ssq_ready
             hmu2_ready hvar_ready hve_ready rs_ready u0_ready u_ready
            base0_ready base_ready f_ready st2_ready mv2_ready ve2_ready rstd2_ready nmr_ready y_ready
            """.split()}
        loaded = [sem("loaded_even"), sem("loaded_odd")]
        stored = [sem("stored_even"), sem("stored_odd")]
        LOADS = 5

        block = ctx.enter_context(nc.Block())

        @block.sync
        def _(sp):
            def load(g):
                rows = bass.ds(g.n * GR, GR)
                sp.dma_start(x_in[:, g.par], x[rows].rearrange("b n d -> n b d")).then_inc(loaded[g.par], 16)
                sp.dma_start(a_in[:, g.par], adj[rows].rearrange("b n e -> n b e")).then_inc(loaded[g.par], 16)
                sp.dma_start(edge_in[:, g.par], adj[rows, 0, :].partition_broadcast(P)).then_inc(loaded[g.par], 16)
                sp.dma_start(mask_in[:, g.par], nodemask[rows].partition_broadcast(P)).then_inc(loaded[g.par], 16)
                sp.dma_start(mrow_in[:, g.par], nodemask[rows]).then_inc(loaded[g.par], 16)

            def load_over(old, new):
                wait(sp, s["mv1_ready"], old.n + 1)
                wait(sp, s["he_ready"], old.n + 1)
                load(new)

            def store(g):
                plain(sp, s["w_loaded"])
                sp.wait_ge(s["y_ready"], g.n * GR + GR)
                sp.dma_start(out[bass.ds(g.n * GR, GR)].rearrange("b n d -> n b d"), y[:, g.par]).then_inc(
                    stored[g.par], 16)

            load(Group(0, 0))
            sp.dma_start(wqk_raw[:], Wqk.rearrange("(c p) a -> p c a", p=P)).then_inc(s["w_loaded"], 16)
            sp.dma_start(wv_raw[:], Wv.rearrange("(c p) a -> p c a", p=P)).then_inc(s["w_loaded"], 16)
            sp.dma_start(w1_raw[:], W1.rearrange("(c p) a -> p c a", p=P)).then_inc(s["w_loaded"], 16)
            sp.dma_start(w2_raw[:], W2.rearrange("(c p) a -> p c a", p=P)).then_inc(s["w_loaded"], 16)
            for i, v in enumerate((b1, gamma, beta)):
                sp.dma_start(vec_rows[i * HC:(i + 1) * HC], v.rearrange("(c p) -> c p", p=P)).then_inc(
                    s["w_loaded"], 16)
            sp.dma_start(b2_rows[:], b2.partition_broadcast(P)).then_inc(s["w_loaded"], 16)
            load(Group(0, 1))
            for k in range(2):
                load_over(Group(0, k), Group(0, k + 2))
            with sp.Fori(1, NG // 2 - 1) as it:
                for k in range(2):
                    store(Group(it - 1, k))
                    load_over(Group(it, k), Group(it, k + 2))
            for k in range(NG - 4, NG):
                store(Group(0, k))
            for par in range(2):
                sp.wait_ge(stored[par], 16 * (NG // 2))

        @block.tensor
        def _(pe):
            def split_product(o, w, m, first, last):
                for j, (a, b) in enumerate(((1, 0), (0, 1), (0, 0))):
                    mm = nc.tensor.matmul(o, w[a], m[b], start=first and j == 0, stop=last and j == 2)
                return mm

            def setup():
                pe.wait_ge(s["w_loaded"], 16 * 8)
                pe.wait_ge(s["ident_ready"], 1)
                nc.tensor.transpose(ps[:, 7, 0:3 * HC], vec_rows[:], ident[0:3 * HC, 0:3 * HC]).then_inc(
                    s["setup_tr"], 1)
                for part in range(2):
                    for a in range(DC):
                        for c in range(DC):
                            mm = nc.tensor.transpose(ps[:, part, a * D + c * P:a * D + (c + 1) * P],
                                                     wqk_raw[:, c, part * D + a * P:part * D + (a + 1) * P], ident[:])
                    mm.then_inc(s["setup_tr"], 1)
                for c in range(DC):
                    for hc in range(HC):
                        mm = nc.tensor.transpose(ps[:, 3 + c, hc * P:(hc + 1) * P],
                                                 w1_raw[:, hc, c * P:(c + 1) * P], ident[:])
                mm.then_inc(s["setup_tr"], 1)
                for hc in range(HC):
                    for c in range(DC):
                        off = (hc % 2) * D + c * P
                        mm = nc.tensor.transpose(ps[:, 5 + hc // 2, off:off + P],
                                                 w2_raw[:, c, hc * P:(hc + 1) * P], ident[:])
                mm.then_inc(s["setup_tr"], 1)
                pe.wait_ge(s["setup_copied"], 2)
                for c in range(DC):
                    for a in range(DC):
                        mm = nc.tensor.matmul(ps[:, 2, c * D:(c + 1) * D], wq_t[:, a, c * P:(c + 1) * P],
                                              wk_t[:, a, :], start=a == 0, stop=a == DC - 1)
                mm.then_inc(s["m_done"], 1)
                pe.wait_ge(s["w2g_ready"], 2)
                pe.wait_ge(s["consts_ready"], 1)
                for hc in range(HC):
                    nc.tensor.matmul(ps[:, 7, 0:D], ones_mean[:], w2_g[:, hc, :], start=hc == 0, stop=hc == HC - 1)
                for hc in range(HC):
                    mm = nc.tensor.matmul(ps[:, 7, D:2 * D], beta_rows[:, hc, :], w2_t[:, hc, :],
                                          start=hc == 0, stop=hc == HC - 1)
                mm.then_inc(s["cb_done"], 1)

            def transpose_inputs(m):
                pe.wait_ge(loaded[m.par], 16 * LOADS * (m.half + 1))
                wait(pe, s["r1_ready"], m.n * GR)
                for c in range(DC):
                    for k in range(GR):
                        mm = nc.tensor.transpose(ps_xt[:, c, k * N:(k + 1) * N],
                                                 x_in[:, m.par, k, c * P:(c + 1) * P], ident[:])
                mm.then_inc(s["xt_done"], 1)

            def transpose_adj(m):
                wait(pe, s["ssq_ready"], m.n - 1)
                for k in range(GR):
                    mm = nc.tensor.transpose(ps_at[:, k, :], a_in[:, m.par, k, :], ident[:])
                mm.then_inc(s["at_done"], 1)

            def t_product(n):
                pe.wait_ge(s["xt_lo_ready"], n.n + 1)
                for co in range(DC):
                    for c in range(DC):
                        mm = split_product(ps_xt[:, co, :],
                                           (m_hi[:, c, co * P:(co + 1) * P], m_lo[:, c, co * P:(co + 1) * P]),
                                           (xt_hi[:, c, :], xt_lo[:, c, :]), c == 0, c == DC - 1)
                mm.then_inc(s["t_done"], 1)

            def s_product(n):
                pe.wait_ge(s["tt_ready"], n.n + 1)
                pe.wait_ge(s["xt_ready"], n.n + 1)
                for k in range(GR):
                    for c in range(DC):
                        mm = nc.tensor.matmul(ps_s[:, k, :], tt[:, c, k * N:(k + 1) * N], xt[:, c, k * N:(k + 1) * N],
                                              start=c == 0, stop=c == DC - 1)
                mm.then_inc(s["s_done"], 1)

            def p_transposes(n):
                pe.wait_ge(s["pn_ready"], n.n + 1)
                pe.wait_ge(s["ht_ready"], n.n + 1)
                for k in range(GR):
                    mm = nc.tensor.transpose(ps_at[:, k, :], pn[:, k, :], ident[:])
                mm.then_inc(s["pt_done"], 1)

            def v_product(n, ks):
                for k in ks:
                    for c in range(DC):
                        mm = split_product(ps_v[:, k, :], (xt_hi[:, c, k * N:(k + 1) * N],
                                                           xt_lo[:, c, k * N:(k + 1) * N]),
                                           (wv_hi[:, c, :], wv_lo[:, c, :]), c == 0, c == DC - 1)
                    mm.then_inc(s["v_done"], 1)

            def w_transpose(n):
                pe.wait_ge(s["w_ready"], n.n * GR + GR)
                nc.tensor.transpose(ps[0:GR, 2, 0:N], w_col[:], ident[:]).then_inc(s["wt_done"], 1)

            def p_transpose(n):
                plain(pe, s["ident_ready"])
                pe.wait_ge(s["prow_ready"], n.n + 1)
                nc.tensor.transpose(ps[:, 2, N:N + GR], p_row[:], ident[0:GR, 0:GR]).then_inc(s["pcol_done"], 1)

            def g_product(n):
                pe.wait_ge(s["rr_ready"], n.n + 1)
                pe.wait_ge(s["pcol_ready"], n.n + 1)
                for k in range(GR):
                    mm = nc.tensor.matmul(ps_s[:, k, :], ht[:, k, :], rr[:, k, :], start=True, stop=True)
                mm.then_inc(s["g_done"], 1)

            def z_product(g):
                pe.wait_ge(s["gp_ready"], g.n + 1)
                wait(pe, s["u0_ready"], g.n * GR)
                for k in range(GR):
                    pe.wait_ge(s["x1_ready"], g.n * GR + k + 1)
                    for c in range(DC):
                        mm = nc.tensor.matmul(ps_zt[:, c, k * N:(k + 1) * N], x1[:, g.par, k, c * P:(c + 1) * P],
                                              gp[:, g.par, k, :], start=True, stop=True)
                mm.then_inc(s["z_done"], 1)

            def w1_product(g):
                pe.wait_ge(s["zt_lo_ready"], g.n + 1)
                for hc in range(HC):
                    if hc == 2:
                        wait(pe, s["f_ready"], g.n)
                    for c in range(DC):
                        mm = split_product(ps[:, W_BANK[hc], :],
                                           (w1_hi[:, c, hc * P:(hc + 1) * P], w1_lo[:, c, hc * P:(hc + 1) * P]),
                                           (zt_hi[:, c, :], zt_lo[:, c, :]), c == 0, c == DC - 1)
                    mm.then_inc(s["w1_done"], 1)

            def w2_product(g, k):
                for hc in range(HC):
                    if k == 0:
                        pe.wait_ge(s["h_lo_ready"], g.n * HC + hc + 1)
                        if hc == 0:
                            pe.wait_ge(s["h_ready"], g.n * HC + 1)
                    if k == 0 and hc == HC - 1:
                        pe.wait_ge(s["h_ready"], g.n * HC + HC)
                    mm = split_product(ps[:, W_BANK[k], 0:W2N],
                                       (h_hi[:, hc, k * N:(k + 1) * N], h_lo[:, hc, k * N:(k + 1) * N]),
                                       (w2_hi[:, hc, :], w2_lo[:, hc, :]), hc == 0, hc == HC - 1)
                mm.then_inc(s["w2_done"], 1)

            def q_transposes(g):
                pe.wait_ge(s["q_ready"], g.n + 1)
                for k in range(GR):
                    mm = nc.tensor.transpose(ps_at[:, k, :], q[:, k * N:(k + 1) * N], ident[:])
                mm.then_inc(s["qt_done"], 1)

            def c2_product(g):
                for k in range(GR):
                    pe.wait_ge(s["u_ready"], g.n * GR + k + 1)
                    mm = nc.tensor.matmul(ps_c2[:, k, :], gp[:, g.par, k, :], u[:, k, :], start=True, stop=True)
                mm.then_inc(s["c2_done"], 1)

            def step(g, n, m, last):
                if g:
                    z_product(g)
                if n:
                    t_product(n)
                if last:
                    c2_product(last)
                if g:
                    w1_product(g)
                if n:
                    s_product(n)
                    p_transposes(n)
                    v_product(n, (0, 1))
                    w_transpose(n)
                    v_product(n, (2, 3))
                if g:
                    w2_product(g, 0)
                if n:
                    p_transpose(n)
                if g:
                    w2_product(g, 1)
                    w2_product(g, 2)
                    if n:
                        pe.wait_ge(s["rr_ready"], n.n + 1)
                    else:
                        pe.wait_ge(s["ssq_ready"], g.n)
                    q_transposes(g)
                    w2_product(g, 3)
                if m:
                    transpose_inputs(m)
                if n:
                    g_product(n)
                if m:
                    transpose_adj(m)

            setup()
            pe.wait_ge(s["setup_act"], 1)
            pe.wait_ge(s["setup_dve"], 1)
            transpose_inputs(Group(0, 0))
            transpose_adj(Group(0, 0))
            step(None, Group(0, 0), Group(0, 1), None)
            step(Group(0, 0), Group(0, 1), Group(0, 2), None)
            step(Group(0, 1), Group(0, 2), Group(0, 3), Group(0, 0))
            with pe.Fori(1, NG // 2 - 1) as it:
                for k in range(2):
                    step(Group(it, k), Group(it, k + 1), Group(it, k + 2), Group(it - 1, k + 1))
            step(Group(0, NG - 2), Group(0, NG - 1), None, Group(0, NG - 3))
            step(Group(0, NG - 1), None, None, Group(0, NG - 2))
            c2_product(Group(0, NG - 1))

        @block.scalar
        def _(act):
            def setup():
                act.wait_ge(s["setup_tr"], 2)
                nc.scalar.copy(wq_t, ps[:, 0, :].rearrange("p (a d) -> p a d", a=DC)).then_inc(s["setup_copied"], 1)
                act.wait_ge(s["w_loaded"], 16 * 8)
                nc.scalar.copy(wv_hi[:], wv_raw[:]).then_inc(s["m_hi_ready"], 1)
                act.wait_ge(s["setup_tr"], 4)
                nc.scalar.copy(w1_hi[:], ps[:, 3:5, :]).then_inc(s["m_hi_ready"], 1)
                act.wait_ge(s["m_done"], 1)
                nc.scalar.copy(m_hi[:], ps[:, 2, :].rearrange("p (a d) -> p a d", a=DC)).then_inc(s["m_hi_ready"], 1)
                act.wait_ge(s["cb_done"], 1)
                act.wait_ge(s["w2c_ready"], 1)
                nc.scalar.copy(cbeta[:], ps[:, 7, D:2 * D]).then_inc(s["m_hi_ready"], 1)
                nc.scalar.copy(w2_hi[:, :, 0:D], w2_c).then_inc(s["setup_act"], 1)

            def zt_high(g):
                act.wait_ge(s["z_done"], g.n + 1)
                nc.scalar.copy(zt_hi[:], ps_zt).then_inc(s["zt_hi_ready"], 1)

            def t_copy(n):
                act.wait_ge(s["t_done"], n.n + 1)
                nc.scalar.copy(tt[:], ps_xt).then_inc(s["tt_ready"], 1)

            def hidden(g):
                for hc in range(HC):
                    act.wait_ge(s["w1_done"], g.n * HC + hc + 1)
                    if hc == 0:
                        wait(act, s["h_lo_ready"], g.n * HC)
                    nc.scalar.activation(h[:, hc, :], ps[:, W_BANK[hc], :], ACT.Relu,
                                         bias=vec_cols[:, hc:hc + 1]).then_inc(s["h_ready"], 1)
                    act.wait_ge(s["h_ready"], g.n * HC + hc + 1)
                    nc.scalar.copy(h_hi[:, hc, :], h[:, hc, :]).then_inc(s["h_hi_ready"], 1)
                wait(act, s["q1_ready"], g.n)
                nc.scalar.activation(sq[:], h[:], ACT.Square).then_inc(s["sq_ready"], 1)

            def final_norm(g):
                act.wait_ge(s["nmr_ready"], g.n + 1)
                wait(act, stored[g.par], 16 * g.half)
                for k in range(GR):
                    nc.scalar.activation(y[:, g.par, k, :], f[:, k, :], ACT.Identity, bias=nmr[:, k:k + 1],
                                         scale=rstd2[:, k:k + 1]).then_inc(s["y_ready"], 1)

            def softmax_exp(n):
                act.wait_ge(s["wbias_ready"], n.n + 1)
                nc.scalar.activation(e_row[:], w_row[:], ACT.Exp, bias=w_bias[:], scale=1.0 / 16.0,
                                     accum_out=e_sum[:]).then_inc(s["e_ready"], 1)

            def u_copy(g):
                for k in range(GR):
                    act.wait_ge(s["w2_done"], g.n * GR + k + 1)
                    if k == 0:
                        wait(act, s["u_ready"], g.n * GR)
                    nc.scalar.copy(u0[:, k, :], ps[:, W_BANK[k], 0:W2N]).then_inc(s["u0_ready"], 1)

            def g_copy(n):
                act.wait_ge(s["g_done"], n.n + 1)
                wait(act, s["c2_done"], n.n - 1)
                nc.scalar.copy(gp[:, n.par], ps_s).then_inc(s["gp_ready"], 1)

            def xt_copy(m):
                act.wait_ge(s["xt_done"], m.n + 1)
                nc.scalar.copy(xt[:], ps_xt).then_inc(s["xt_ready"], 1)

            def xt_high(m):
                act.wait_ge(s["xt_ready"], m.n + 1)
                nc.scalar.copy(xt_hi[:], xt[:]).then_inc(s["xt_hi_ready"], 1)

            def step(g, n, m, last):
                if g:
                    zt_high(g)
                if n:
                    t_copy(n)
                if g:
                    hidden(g)
                if n:
                    softmax_exp(n)
                if last:
                    final_norm(last)
                if g:
                    u_copy(g)
                if m:
                    xt_copy(m)
                if n:
                    g_copy(n)
                if m:
                    xt_high(m)

            setup()
            xt_copy(Group(0, 0))
            xt_high(Group(0, 0))
            step(None, Group(0, 0), Group(0, 1), None)
            step(Group(0, 0), Group(0, 1), Group(0, 2), None)
            step(Group(0, 1), Group(0, 2), Group(0, 3), Group(0, 0))
            with act.Fori(1, NG // 2 - 1) as it:
                for k in range(2):
                    step(Group(it, k), Group(it, k + 1), Group(it, k + 2), Group(it - 1, k + 1))
            step(Group(0, NG - 2), Group(0, NG - 1), None, Group(0, NG - 3))
            step(Group(0, NG - 1), None, None, Group(0, NG - 2))
            final_norm(Group(0, NG - 1))

        @block.vector
        def _(dve):
            V = nc.vector

            def setup():
                dve.wait_ge(s["setup_tr"], 1)
                V.tensor_copy(vec_cols[:], ps[:, 7, 0:3 * HC]).then_inc(s["vec_ready"], 1)
                dve.wait_ge(s["setup_tr"], 3)
                V.tensor_copy(wk_t, ps[:, 1, :].rearrange("p (a d) -> p a d", a=DC)).then_inc(s["setup_copied"], 1)
                dve.wait_ge(s["setup_tr"], 5)
                dve.wait_ge(s["vec_ready"], 1)
                dve.wait_ge(s["consts_ready"], 1)
                V.tensor_copy(w2_t, ps[:, 5:7, :].rearrange("p a (b d) -> p (a b) d", d=D)).then_inc(s["w2g_ready"], 1)
                for hc in range(HC):
                    V.tensor_scalar(beta_rows[:, hc, :], ones_mean[:], vec_cols[:, 2 * HC + hc:2 * HC + hc + 1],
                                    float(DH), ALU.mult, ALU.mult)
                for hc in range(HC):
                    off = (hc % 2) * D
                    ins = V.tensor_scalar(w2_g[:, hc, :], ps[:, 5 + hc // 2, off:off + D],
                                          vec_cols[:, HC + hc:HC + hc + 1], None, ALU.mult)
                ins.then_inc(s["w2g_ready"], 1)
                dve.wait_ge(s["m_hi_ready"], 2)
                V.tensor_tensor(wv_lo[:], wv_raw[:], wv_hi[:].bitcast(F32), ALU.subtract)
                V.tensor_tensor(w1_lo[:], ps[:, 3:5, :], w1_hi[:].bitcast(F32), ALU.subtract)
                dve.wait_ge(s["m_hi_ready"], 3)
                V.tensor_tensor(m_lo[:], ps[:, 2, :].rearrange("p (a d) -> p a d", a=DC), m_hi[:].bitcast(F32),
                                ALU.subtract)
                dve.wait_ge(s["cb_done"], 1)
                dve.wait_ge(s["w2g_ready"], 2)
                V.tensor_tensor(w2_c, w2_g, ps[:, 7, 0:D].unsqueeze(1).to_broadcast([P, HC, D]),
                                ALU.subtract).then_inc(s["w2c_ready"], 1)
                dve.wait_ge(s["setup_act"], 1)
                dve.wait_ge(s["w2c_ready"], 1)
                V.tensor_tensor(w2_lo[:, :, 0:D], w2_c, w2_hi[:, :, 0:D].bitcast(F32),
                                ALU.subtract).then_inc(s["setup_dve"], 1)

            def xt_low(m):
                dve.wait_ge(s["xt_hi_ready"], m.n + 1)
                V.tensor_tensor(xt_lo[:], xt[:], xt_hi[:].bitcast(F32), ALU.subtract).then_inc(s["xt_lo_ready"], 1)

            def final_stats(g):
                dve.wait_ge(s["c2_done"], g.n + 1)
                dve.wait_ge(s["base_ready"], g.n + 1)
                wait(dve, s["y_ready"], g.n * GR)
                V.tensor_tensor(f[:], ps_c2, base[:], ALU.add).then_inc(s["f_ready"], 1)
                dve.wait_ge(s["f_ready"], g.n + 1)
                for k in range(GR):
                    ins = V.bn_stats(st2[:, k, :], f[:, k, :])
                ins.then_inc(s["st2_ready"], 1)
                plain(dve, s["vec_ready"])
                dve.wait_ge(s["st2_ready"], g.n + 1)
                for k in range(GR):
                    ins = V.bn_aggr(mv2[:, k, :], st2[:, k, :])
                ins.then_inc(s["mv2_ready"], 1)
                dve.wait_ge(s["mv2_ready"], g.n + 1)
                V.tensor_scalar(ve2[:], mv2[:, :, 1], EPS, None, ALU.add).then_inc(s["ve2_ready"], 1)

            def final_bias(g):
                dve.wait_ge(s["rstd2_ready"], g.n + 1)
                V.scalar_tensor_tensor(out=nmr[:], in0=mv2[:, :, 0], scalar=-1.0, in1=rstd2[:], op0=ALU.mult,
                                       op1=ALU.mult).then_inc(s["nmr_ready"], 1)

            def zt_low(g):
                dve.wait_ge(s["zt_hi_ready"], g.n + 1)
                V.tensor_tensor(zt_lo[:], ps_zt, zt_hi[:].bitcast(F32), ALU.subtract).then_inc(s["zt_lo_ready"], 1)

            def incidence(n):
                dve.wait_ge(loaded[n.par], 16 * LOADS * (n.half + 1))
                wait(dve, s["pn_ready"], n.n)
                V.tensor_scalar(hn[:], a_in[:, n.par], 0.0, None, ALU.not_equal).then_inc(s["hn_ready"], 1)
                dve.wait_ge(s["at_done"], n.n + 1)
                wait(dve, s["g_done"], n.n)
                V.tensor_scalar(ht[:], ps_at, 0.0, None, ALU.not_equal).then_inc(s["ht_ready"], 1)
                dve.wait_ge(s["ht_ready"], n.n + 1)
                V.tensor_reduce(cnt[:], ht[:], AX_X, ALU.add).then_inc(s["cnt_ready"], 1)
                dve.wait_ge(s["cnt_ready"], n.n + 1)
                V.tensor_scalar(cnt1[:], cnt[:], 1.0, None, ALU.max).then_inc(s["cnt1_ready"], 1)
                dve.wait_ge(s["cnt1_ready"], n.n + 1)
                V.reciprocal(be[:], cnt1[:]).then_inc(s["be_ready"], 1)

            def degrees(n):
                dve.wait_ge(s["he_ready"], n.n + 1)
                V.tensor_reduce(deg[:], he[:], AX_X, ALU.add).then_inc(s["deg_ready"], 1)
                dve.wait_ge(s["deg_ready"], n.n + 1)
                V.scalar_tensor_tensor(out=deg1[:], in0=deg[:], scalar=0.0, in1=deg[:], op0=ALU.is_le,
                                       op1=ALU.max).then_inc(s["deg1_ready"], 1)
                dve.wait_ge(s["deg1_ready"], n.n + 1)
                V.reciprocal(deg_inv[:], deg1[:]).then_inc(s["dinv_ready"], 1)
                dve.wait_ge(s["dinv_ready"], n.n + 1)
                V.scalar_tensor_tensor(out=dn[:], in0=deg[:], scalar=0.0, in1=deg_inv[:], op0=ALU.is_gt,
                                       op1=ALU.mult).then_inc(s["dn_ready"], 1)

            def hidden_low(g, hc):
                dve.wait_ge(s["h_hi_ready"], g.n * HC + hc + 1)
                V.tensor_tensor(h_lo[:, hc, :], h[:, hc, :], h_hi[:, hc, :].bitcast(F32),
                                ALU.subtract).then_inc(s["h_lo_ready"], 1)

            def dots(n):
                dve.wait_ge(s["am_ready"], n.n + 1)
                dve.wait_ge(s["s_done"], n.n + 1)
                for k in range(GR):
                    V.tensor_tensor_reduce(dot_junk[:, k, :], ps_s[:, k, :], am[:, k, :], 1.0, 0.0, ALU.mult, ALU.add,
                                           w_col[:, k:k + 1]).then_inc(s["w_ready"], 1)

            def r_scale(n):
                dve.wait_ge(s["pt_done"], n.n + 1)
                dve.wait_ge(s["be_ready"], n.n + 1)
                V.tensor_tensor(rr[:], ps_at, be[:].unsqueeze(2).to_broadcast([P, GR, N]),
                                ALU.mult).then_inc(s["rr_ready"], 1)

            def softmax_max(n):
                dve.wait_ge(s["wt_done"], n.n + 1)
                V.tensor_tensor(w_row[:], ps[0:GR, 2, 0:N], mrow_in[:, n.par], ALU.mult).then_inc(s["wrow_ready"], 1)
                dve.wait_ge(s["wrow_ready"], n.n + 1)
                V.tensor_reduce(w_max[:], w_row[:], AX_X, ALU.max).then_inc(s["wmax_ready"], 1)
                dve.wait_ge(s["wmax_ready"], n.n + 1)
                V.tensor_scalar(w_bias[:], w_max[:], -1.0 / 16.0, None, ALU.mult).then_inc(s["wbias_ready"], 1)

            def softmax_scale(n):
                dve.wait_ge(s["e_ready"], n.n + 1)
                V.reciprocal(e_inv[:], e_sum[:]).then_inc(s["einv_ready"], 1)
                dve.wait_ge(s["einv_ready"], n.n + 1)
                V.tensor_scalar(p_row[:], e_row[:], e_inv[:], None, ALU.mult).then_inc(s["prow_ready"], 1)

            def residual(n):
                dve.wait_ge(s["pcol_done"], n.n + 1)
                V.tensor_copy(p_col[:], ps[:, 2, N:N + GR]).then_inc(s["pcol_ready"], 1)
                dve.wait_ge(s["pcol_ready"], n.n + 1)
                for k in range(GR):
                    dve.wait_ge(s["v_done"], n.n * GR + k + 1)
                    V.scalar_tensor_tensor(out=r1[:, k, :], in0=ps_v[:, k, :], scalar=p_col[:, k:k + 1],
                                           in1=x_in[:, n.par, k, :], op0=ALU.mult,
                                           op1=ALU.add).then_inc(s["r1_ready"], 1)

            def x1_stats(n):
                for k in range(GR):
                    dve.wait_ge(s["r1_ready"], n.n * GR + k + 1)
                    V.bn_stats(st1[:, k, :], r1[:, k, :]).then_inc(s["st1_ready"], 1)

            def x1_aggregate(n):
                plain(dve, s["vec_ready"])
                dve.wait_ge(s["st1_ready"], n.n * GR + GR)
                for k in range(GR):
                    ins = V.bn_aggr(mv1[:, k, :], st1[:, k, :])
                ins.then_inc(s["mv1_ready"], 1)
                dve.wait_ge(s["mv1_ready"], n.n + 1)
                V.tensor_scalar(ve1[:], mv1[:, :, 1], EPS, None, ALU.add).then_inc(s["ve1_ready"], 1)

            def x1_apply(n):
                dve.wait_ge(s["rstd1_ready"], n.n + 1)
                wait(dve, s["base_ready"], n.n - 1)
                for k in range(GR):
                    V.tensor_scalar(x1[:, n.par, k, :], r1[:, k, :], mv1[:, k, 0:1], rstd1[:, k:k + 1],
                                    ALU.subtract, ALU.mult).then_inc(s["x1_ready"], 1)

            def square_sums(g):
                dve.wait_ge(s["qt_done"], g.n + 1)
                V.tensor_reduce(ssq[:], ps_at, AX_X, ALU.add).then_inc(s["ssq_ready"], 1)

            def hidden_stats(g):
                dve.wait_ge(s["u0_ready"], g.n * GR + GR)
                V.scalar_tensor_tensor(out=hmu2[:], in0=u0[:, :, D], scalar=-1.0, in1=u0[:, :, D],
                                       op0=ALU.mult, op1=ALU.mult).then_inc(s["hmu2_ready"], 1)
                dve.wait_ge(s["hmu2_ready"], g.n + 1)
                V.scalar_tensor_tensor(out=hvar[:], in0=ssq[:], scalar=1.0 / DH, in1=hmu2[:], op0=ALU.mult,
                                       op1=ALU.add).then_inc(s["hvar_ready"], 1)
                dve.wait_ge(s["hvar_ready"], g.n + 1)
                V.tensor_scalar(hve[:], hvar[:], 0.0, EPS, ALU.max, ALU.add).then_inc(s["hve_ready"], 1)

            def u_rows(g):
                dve.wait_ge(s["rs_ready"], g.n + 1)
                wait(dve, s["c2_done"], g.n)
                for k in range(GR):
                    V.scalar_tensor_tensor(out=u[:, k, :], in0=u0[:, k, 0:D], scalar=rs[:, k:k + 1], in1=cbeta[:],
                                           op0=ALU.mult, op1=ALU.add).then_inc(s["u_ready"], 1)

            def step(g, n, m, last):
                if g:
                    zt_low(g)
                if n:
                    incidence(n)
                if last:
                    final_stats(last)
                if g:
                    hidden_low(g, 0)
                if n:
                    degrees(n)
                if g:
                    for hc in range(1, HC):
                        hidden_low(g, hc)
                if last:
                    final_bias(last)
                if n:
                    dots(n)
                    r_scale(n)
                    softmax_max(n)
                    softmax_scale(n)
                    residual(n)
                    x1_stats(n)
                    x1_aggregate(n)
                if g:
                    square_sums(g)
                if n:
                    x1_apply(n)
                if g:
                    hidden_stats(g)
                if m:
                    xt_low(m)
                if g:
                    u_rows(g)

            setup()
            xt_low(Group(0, 0))
            step(None, Group(0, 0), Group(0, 1), None)
            step(Group(0, 0), Group(0, 1), Group(0, 2), None)
            step(Group(0, 1), Group(0, 2), Group(0, 3), Group(0, 0))
            with dve.Fori(1, NG // 2 - 1) as it:
                for k in range(2):
                    step(Group(it, k), Group(it, k + 1), Group(it, k + 2), Group(it - 1, k + 1))
            step(Group(0, NG - 2), Group(0, NG - 1), None, Group(0, NG - 3))
            step(Group(0, NG - 1), None, None, Group(0, NG - 2))
            final_stats(Group(0, NG - 1))
            final_bias(Group(0, NG - 1))

        @block.gpsimd
        def _(pool):
            Q = nc.gpsimd

            def setup():
                Q.memset(ident[:], 0.0).then_inc(s["ident_zero"], 1)
                pool.wait_ge(s["ident_zero"], 1)
                Q.affine_select(out=ident[:], in_=ident[:], compare_op=ALU.not_equal, fill=1.0, base=0,
                                pattern=[[-1, P]], channel_multiplier=1).then_inc(s["ident_ready"], 1)
                Q.memset(neg_half[:], -0.5)
                Q.memset(w2_hi[:, :, D:W2N].bitcast(F32), 1.0 / DH)
                Q.memset(w2_lo[:, :, D:W2N].bitcast(F32), 0.0)
                Q.memset(ones_mean[:], 1.0 / DH).then_inc(s["consts_ready"], 1)
                pool.wait_ge(s["consts_ready"], 1)

            def masked_adj(n):
                pool.wait_ge(loaded[n.par], 16 * LOADS * (n.half + 1))
                wait(pool, s["w_ready"], n.n * GR)
                Q.tensor_tensor(am[:], a_in[:, n.par], mask_in[:, n.par], ALU.mult).then_inc(s["am_ready"], 1)

            def base_rows(g):
                pool.wait_ge(s["x1_ready"], g.n * GR + GR)
                Q.tensor_tensor(base0[:], x1[:, g.par], b2_rows[:].unsqueeze(1).to_broadcast([P, GR, D]),
                                ALU.add).then_inc(s["base0_ready"], 1)
                pool.wait_ge(s["base0_ready"], g.n + 1)
                wait(pool, s["f_ready"], g.n)
                Q.tensor_tensor(base[:], base0[:], x1[:, g.par], ALU.add).then_inc(s["base_ready"], 1)

            def final_rstd(g):
                pool.wait_ge(s["ve2_ready"], g.n + 1)
                wait(pool, s["y_ready"], g.n * GR)
                Q.tensor_tensor(rstd2[:], ve2[:], neg_half[:], ALU.pow).then_inc(s["rstd2_ready"], 1)

            def edge_weights(n):
                pool.wait_ge(s["hn_ready"], n.n + 1)
                wait(pool, s["deg_ready"], n.n)
                Q.tensor_tensor(he[:], hn[:], edge_in[:, n.par], ALU.mult).then_inc(s["he_ready"], 1)

            def scaled_incidence(n):
                pool.wait_ge(s["dn_ready"], n.n + 1)
                wait(pool, s["pt_done"], n.n)
                Q.tensor_tensor(pn[:], hn[:], dn[:].unsqueeze(2).to_broadcast([P, GR, N]),
                                ALU.mult).then_inc(s["pn_ready"], 1)

            def square_blocks(g):
                pool.wait_ge(s["sq_ready"], g.n + 1)
                Q.tensor_tensor(q1[:], sq[:, 0:2, :], sq[:, 2:4, :], ALU.add).then_inc(s["q1_ready"], 1)
                pool.wait_ge(s["q1_ready"], g.n + 1)
                wait(pool, s["qt_done"], g.n)
                Q.tensor_tensor(q[:], q1[:, 0, :], q1[:, 1, :], ALU.add).then_inc(s["q_ready"], 1)

            def hidden_rstd(g):
                pool.wait_ge(s["hve_ready"], g.n + 1)
                wait(pool, s["u_ready"], g.n * GR)
                Q.tensor_tensor(rs[:], hve[:], neg_half[:], ALU.pow).then_inc(s["rs_ready"], 1)

            def x1_rstd(n):
                pool.wait_ge(s["ve1_ready"], n.n + 1)
                Q.tensor_tensor(rstd1[:], ve1[:], neg_half[:], ALU.pow).then_inc(s["rstd1_ready"], 1)

            def step(g, n, last):
                if n:
                    masked_adj(n)
                    edge_weights(n)
                    scaled_incidence(n)
                if last:
                    final_rstd(last)
                if g:
                    base_rows(g)
                    square_blocks(g)
                if n:
                    x1_rstd(n)
                if g:
                    hidden_rstd(g)

            setup()
            pool.wait_ge(s["w_loaded"], 16 * 8)
            step(None, Group(0, 0), None)
            step(Group(0, 0), Group(0, 1), None)
            step(Group(0, 1), Group(0, 2), Group(0, 0))
            with pool.Fori(1, NG // 2 - 1) as it:
                for k in range(2):
                    step(Group(it, k), Group(it, k + 1), Group(it - 1, k + 1))
            step(Group(0, NG - 2), Group(0, NG - 1), Group(0, NG - 3))
            step(Group(0, NG - 1), None, Group(0, NG - 2))
            final_rstd(Group(0, NG - 1))


_INS = ['x', 'adj', 'nodemask', 'L0_gnn_Wqk', 'L0_gnn_Wv', 'L1_gnn_W1', 'L1_gnn_b1', 'L1_gnn_gamma', 'L1_gnn_beta',
        'L1_gnn_W2', 'L1_gnn_b2']


def kernel(**inputs):
    import numpy as _np
    import concourse.bacc as _bacc
    from concourse import mybir as _mybir
    from concourse.bass_utils import run_bass_kernel_spmd as _run

    nc = _bacc.Bacc("TRN2", target_bir_lowering=False, num_devices=1)
    arrays, args = {}, []
    for name in _INS:
        a = _np.ascontiguousarray(inputs[name])
        arrays[f"in_{name}"] = a
        args.append(nc.dram_tensor(f"in_{name}", a.shape, _mybir.dt.from_np(a.dtype), kind="ExternalInput").ap())
    shape = inputs['x'].shape
    args.append(nc.dram_tensor("out_x", shape, _mybir.dt.float32, kind="ExternalOutput").ap())
    build_program(nc, *args)
    r = _run(nc, [arrays], core_ids=[0])
    return r.results[0]["out_x"]
```

```python
from contextlib import ExitStack

import concourse.bass as bass
from concourse import mybir

ALU = mybir.AluOpType
ACT = mybir.ActivationFunctionType
F32 = mybir.dt.float32
F32R = mybir.dt.float32r
AX_X = mybir.AxisListType.X
P = 128
EPS = 1e-5


class Group:

    def __init__(self, it, k):
        self.n = it * 2 + k
        self.half = it + k // 2
        self.par = k % 2


def wait(eng, sem, value):
    if isinstance(value, int) and value <= 0:
        return
    eng.wait_ge(sem, value)


def plain(eng, sem):
    eng.wait_ge(sem, 1)


def build_program(nc, x, adj, nodemask, Wqk, Wv, W1, b1, gamma, beta, W2, b2, out):
    B, N, D = x.shape
    DH = W1.shape[0]
    GR = 4
    NG = B // GR
    DC = D // P
    HC = DH // P
    GN = GR * N
    W2N = D + 2
    assert N == P and DC == 2 and HC == 4 and GN == 512 and NG % 2 == 0

    with ExitStack() as ctx:
        def sb(name, shape, dt=F32):
            return ctx.enter_context(nc.sbuf_tensor(name, shape, dt))

        def sem(name):
            return ctx.enter_context(nc.semaphore(name))

        ident = sb("ident", [P, P])
        neg_half = sb("neg_half", [P, GR])
        ones_mean = sb("ones_mean", [P, P])
        b2_rows = sb("b2_rows", [P, D])
        cbeta = sb("cbeta", [P, D])
        vec_rows = sb("vec_rows", [3 * HC, P])
        vec_cols = sb("vec_cols", [P, 3 * HC])
        m_hi, m_lo = sb("m_hi", [P, DC, D], F32R), sb("m_lo", [P, DC, D], F32R)
        wv_hi, wv_lo = sb("wv_hi", [P, DC, D], F32R), sb("wv_lo", [P, DC, D], F32R)
        w1_hi, w1_lo = sb("w1_hi", [P, DC, DH], F32R), sb("w1_lo", [P, DC, DH], F32R)
        w2_hi, w2_lo = sb("w2_hi", [P, HC, W2N], F32R), sb("w2_lo", [P, HC, W2N], F32R)

        x_in = sb("x_in", [P, 2, GR, D])
        a_in = sb("a_in", [P, 2, GR, N])
        mask_in = sb("mask_in", [P, 2, GR, N])
        edge_in = sb("edge_in", [P, 2, GR, N])
        mrow_in = sb("mrow_in", [GR, 2, N])
        xt = sb("xt", [P, DC, GN])
        xt_hi, xt_lo = sb("xt_hi", [P, DC, GN], F32R), sb("xt_lo", [P, DC, GN], F32R)
        tt = sb("tt", [P, DC, GN])
        am = sb("am", [P, GR, N])
        dot_junk = sb("dot_junk", [P, GR, N])
        w_col = sb("w_col", [P, GR])
        w_row = sb("w_row", [GR, N])
        w_max = sb("w_max", [GR, 1])
        w_bias = sb("w_bias", [GR, 1])
        e_row = sb("e_row", [GR, N])
        e_sum = sb("e_sum", [GR, 1])
        e_inv = sb("e_inv", [GR, 1])
        p_row = sb("p_row", [GR, N])
        p_col = sb("p_col", [P, GR])
        hn = sb("hn", [P, GR, N])
        ht = sb("ht", [P, GR, N])
        he = sb("he", [P, GR, N])
        pn = sb("pn", [P, GR, N])
        rr = sb("rr", [P, GR, N])
        cnt = sb("cnt", [P, GR])
        cnt1 = sb("cnt1", [P, GR])
        be = sb("be", [P, GR])
        deg = sb("deg", [P, GR])
        deg1 = sb("deg1", [P, GR])
        deg_inv = sb("deg_inv", [P, GR])
        dn = sb("dn", [P, GR])
        gp = sb("gp", [P, 2, GR, N])
        r1 = sb("r1", [P, GR, D])
        st1 = sb("st1", [P, GR, 6])
        mv1 = sb("mv1", [P, GR, 2])
        ve1 = sb("ve1", [P, GR])
        rstd1 = sb("rstd1", [P, GR])
        x1 = sb("x1", [P, 2, GR, D])
        zt_hi, zt_lo = sb("zt_hi", [P, DC, GN], F32R), sb("zt_lo", [P, DC, GN], F32R)
        h = sb("h", [P, HC, GN])
        h_hi, h_lo = sb("h_hi", [P, HC, GN], F32R), sb("h_lo", [P, HC, GN], F32R)
        sq = sb("sq", [P, HC, GN])
        q1 = sb("q1", [P, 2, GN])
        q = sb("q", [P, GN])
        ssq = sb("ssq", [P, GR])
        hmu2 = sb("hmu2", [P, GR])
        hvar = sb("hvar", [P, GR])
        hve = sb("hve", [P, GR])
        rs = sb("rs", [P, GR])
        u0 = sb("u0", [P, GR, W2N])
        u = sb("u", [P, GR, D])
        base0 = sb("base0", [P, GR, D])
        base = sb("base", [P, GR, D])
        f = sb("f", [P, GR, D])
        st2 = sb("st2", [P, GR, 6])
        mv2 = sb("mv2", [P, GR, 2])
        ve2 = sb("ve2", [P, GR])
        rstd2 = sb("rstd2", [P, GR])
        nmr = sb("nmr", [P, GR])
        y = sb("y", [P, 2, GR, D])

        wqk_raw = sb("wqk_raw", [P, DC, 2 * D])
        wv_raw = sb("wv_raw", [P, DC, D])
        w1_raw = sb("w1_raw", [P, HC, D])
        w2_raw = sb("w2_raw", [P, DC, DH])
        wq_t = h[:, 0, :].rearrange("p (a d) -> p a d", a=DC)
        wk_t = h[:, 1, :].rearrange("p (a d) -> p a d", a=DC)
        w2_t = sq[:, 0:2, :].rearrange("p a (b d) -> p (a b) d", d=D)
        w2_g = sq[:, 2:4, :].rearrange("p a (b d) -> p (a b) d", d=D)
        w2_c = h[:, 2:4, :].rearrange("p a (b d) -> p (a b) d", d=D)
        beta_rows = f[:, 0:2, :].rearrange("p a (b d) -> p (a b) d", d=P)

        ps = ctx.enter_context(nc.psum_tensor("ps", [P, 8, 512], F32))
        X_T, A_T, SMALL = (0, 2), 3, 2
        ps_xt = ps[:, 0:2, :]
        ps_v = ps[:, 0:2, :].rearrange("p a (b d) -> p (a b) d", d=D)
        ps_s = ps[:, 2, :].rearrange("p (g n) -> p g n", g=GR)
        ps_at = ps[:, 3, :].rearrange("p (g n) -> p g n", g=GR)
        ps_zt = ps[:, 4:6, :]
        W_BANK = (4, 5, 6, 7)
        ps_c2 = ps[:, 6:8, :].rearrange("p a (b d) -> p (a b) d", d=D)

        s = {name: sem(name) for name in """
            wqk_loaded wv_loaded w12_loaded ident_zero ident_ready consts_ready setup_tr setup_copied m_done
            m_hi_ready m_lo_ready wv_hi_ready wv_lo_ready w1_hi_ready w1_lo_ready w2_hi_ready w2_lo_ready
            vec_ready w2t_ready w2g_ready cb_done w2c_ready cbeta_ready
            xt_done at_done t_done s_done pt_done v_done wt_done pcol_done g_done z_done w1_done w2_done qt_done c2_done
            xt_ready xt_hi_ready xt_lo_ready tt_ready am_ready w_ready wrow_ready wmax_ready wbias_ready e_ready
            einv_ready prow_ready pcol_ready
            hn_ready ht_ready cnt_ready cnt1_ready be_ready he_ready deg_ready deg1_ready dinv_ready dn_ready pn_ready
            rr_ready gp_ready r1_ready st1_ready mv1_ready ve1_ready rstd1_ready x1_ready
            zt_hi_ready zt_lo_ready h_ready h_hi_ready h_lo_ready sq_ready q1_ready q_ready ssq_ready
             hmu2_ready hvar_ready hve_ready rs_ready u0_ready u_ready
            base0_ready base_ready f_ready st2_ready mv2_ready ve2_ready rstd2_ready nmr_ready y_ready
            """.split()}
        loaded = [sem("loaded_even"), sem("loaded_odd")]
        stored = [sem("stored_even"), sem("stored_odd")]
        LOADS = 5

        block = ctx.enter_context(nc.Block())

        @block.sync
        def _(sp):
            def load(g):
                rows = bass.ds(g.n * GR, GR)
                sp.dma_start(x_in[:, g.par], x[rows].rearrange("b n d -> n b d")).then_inc(loaded[g.par], 16)
                sp.dma_start(a_in[:, g.par], adj[rows].rearrange("b n e -> n b e")).then_inc(loaded[g.par], 16)
                sp.dma_start(edge_in[:, g.par], adj[rows, 0, :].partition_broadcast(P)).then_inc(loaded[g.par], 16)
                sp.dma_start(mask_in[:, g.par], nodemask[rows].partition_broadcast(P)).then_inc(loaded[g.par], 16)
                sp.dma_start(mrow_in[:, g.par], nodemask[rows]).then_inc(loaded[g.par], 16)

            def load_over(old, new):
                wait(sp, s["mv1_ready"], old.n + 1)
                wait(sp, s["he_ready"], old.n + 1)
                load(new)

            def store(g):
                plain(sp, loaded[0])
                sp.wait_ge(s["y_ready"], g.n * GR + GR)
                sp.dma_start(out[bass.ds(g.n * GR, GR)].rearrange("b n d -> n b d"), y[:, g.par]).then_inc(
                    stored[g.par], 16)

            load(Group(0, 0))
            load(Group(0, 1))
            for k in range(2):
                load_over(Group(0, k), Group(0, k + 2))
            with sp.Fori(1, NG // 2 - 1) as it:
                for k in range(2):
                    store(Group(it - 1, k))
                    load_over(Group(it, k), Group(it, k + 2))
            for k in range(NG - 4, NG):
                store(Group(0, k))
            for par in range(2):
                sp.wait_ge(stored[par], 16 * (NG // 2))

        @block.tensor
        def _(pe):
            def split_product(o, w, m, first, last):
                for j, (a, b) in enumerate(((1, 0), (0, 1), (0, 0))):
                    mm = nc.tensor.matmul(o, w[a], m[b], start=first and j == 0, stop=last and j == 2)
                return mm

            def wqk_transposes():
                pe.wait_ge(s["ident_ready"], 1)
                pe.wait_ge(s["wqk_loaded"], 16)
                for part in range(2):
                    for a in range(DC):
                        for c in range(DC):
                            mm = nc.tensor.transpose(ps[:, 4 + part, a * D + c * P:a * D + (c + 1) * P],
                                                     wqk_raw[:, c, part * D + a * P:part * D + (a + 1) * P], ident[:])
                    mm.then_inc(s["setup_tr"], 1)

            def m_product():
                pe.wait_ge(s["setup_copied"], 2)
                for c in range(DC):
                    for a in range(DC):
                        mm = nc.tensor.matmul(ps[:, 6, c * D:(c + 1) * D], wq_t[:, a, c * P:(c + 1) * P],
                                              wk_t[:, a, :], start=a == 0, stop=a == DC - 1)
                mm.then_inc(s["m_done"], 1)

            def w1_transposes():
                pe.wait_ge(s["w12_loaded"], 16 * 6)
                nc.tensor.transpose(ps[:, 7, 0:3 * HC], vec_rows[:], ident[0:3 * HC, 0:3 * HC]).then_inc(
                    s["setup_tr"], 1)
                for c in range(DC):
                    for hc in range(HC):
                        mm = nc.tensor.transpose(ps[:, 4 + c, hc * P:(hc + 1) * P],
                                                 w1_raw[:, hc, c * P:(c + 1) * P], ident[:])
                mm.then_inc(s["setup_tr"], 1)

            def w2_transposes():
                pe.wait_ge(s["vec_ready"], 1)
                for hc in range(HC):
                    for c in range(DC):
                        off = (hc % 2) * D + c * P
                        mm = nc.tensor.transpose(ps[:, 6 + hc // 2, off:off + P],
                                                 w2_raw[:, c, hc * P:(hc + 1) * P], ident[:])
                mm.then_inc(s["setup_tr"], 1)

            def w2_constants():
                pe.wait_ge(s["w1_lo_ready"], 1)
                pe.wait_ge(s["w2t_ready"], 1)
                pe.wait_ge(s["w2g_ready"], 1)
                pe.wait_ge(s["consts_ready"], 1)
                for hc in range(HC):
                    nc.tensor.matmul(ps[:, 4, 0:D], ones_mean[:], w2_g[:, hc, :], start=hc == 0, stop=hc == HC - 1)
                for hc in range(HC):
                    mm = nc.tensor.matmul(ps[:, 5, 0:D], beta_rows[:, hc, :], w2_t[:, hc, :],
                                          start=hc == 0, stop=hc == HC - 1)
                mm.then_inc(s["cb_done"], 1)

            def transpose_inputs(m):
                pe.wait_ge(loaded[m.par], 16 * LOADS * (m.half + 1))
                wait(pe, s["r1_ready"], m.n * GR)
                for c in range(DC):
                    for k in range(GR):
                        mm = nc.tensor.transpose(ps_xt[:, c, k * N:(k + 1) * N],
                                                 x_in[:, m.par, k, c * P:(c + 1) * P], ident[:])
                    mm.then_inc(s["xt_done"], 1)

            def transpose_adj(m):
                wait(pe, s["ssq_ready"], m.n - 1)
                for k in range(GR):
                    mm = nc.tensor.transpose(ps_at[:, k, :], a_in[:, m.par, k, :], ident[:])
                mm.then_inc(s["at_done"], 1)

            def t_product(n):
                pe.wait_ge(s["xt_ready"], n.n * DC + DC)
                for c in range(DC):
                    pe.wait_ge(s["xt_lo_ready"], n.n * DC + c + 1)
                    for co in range(DC):
                        mm = split_product(ps_xt[:, co, :],
                                           (m_hi[:, c, co * P:(co + 1) * P], m_lo[:, c, co * P:(co + 1) * P]),
                                           (xt_hi[:, c, :], xt_lo[:, c, :]), c == 0, c == DC - 1)
                mm.then_inc(s["t_done"], 1)

            def s_product(n):
                pe.wait_ge(s["tt_ready"], n.n + 1)
                pe.wait_ge(s["xt_ready"], n.n * DC + DC)
                for k in range(GR):
                    for c in range(DC):
                        mm = nc.tensor.matmul(ps_s[:, k, :], tt[:, c, k * N:(k + 1) * N], xt[:, c, k * N:(k + 1) * N],
                                              start=c == 0, stop=c == DC - 1)
                mm.then_inc(s["s_done"], 1)

            def p_transposes(n):
                pe.wait_ge(s["pn_ready"], n.n + 1)
                pe.wait_ge(s["ht_ready"], n.n + 1)
                for k in range(GR):
                    mm = nc.tensor.transpose(ps_at[:, k, :], pn[:, k, :], ident[:])
                mm.then_inc(s["pt_done"], 1)

            def v_product(n, ks):
                for k in ks:
                    for c in range(DC):
                        mm = split_product(ps_v[:, k, :], (xt_hi[:, c, k * N:(k + 1) * N],
                                                           xt_lo[:, c, k * N:(k + 1) * N]),
                                           (wv_hi[:, c, :], wv_lo[:, c, :]), c == 0, c == DC - 1)
                    mm.then_inc(s["v_done"], 1)

            def w_transpose(n):
                pe.wait_ge(s["w_ready"], n.n * GR + GR)
                nc.tensor.transpose(ps[0:GR, 2, 0:N], w_col[:], ident[:]).then_inc(s["wt_done"], 1)

            def p_transpose(n):
                plain(pe, s["ident_ready"])
                pe.wait_ge(s["prow_ready"], n.n + 1)
                nc.tensor.transpose(ps[:, 2, N:N + GR], p_row[:], ident[0:GR, 0:GR]).then_inc(s["pcol_done"], 1)

            def g_product(n):
                pe.wait_ge(s["rr_ready"], n.n + 1)
                pe.wait_ge(s["pcol_ready"], n.n + 1)
                for k in range(GR):
                    mm = nc.tensor.matmul(ps_s[:, k, :], ht[:, k, :], rr[:, k, :], start=True, stop=True)
                mm.then_inc(s["g_done"], 1)

            def z_product(g):
                pe.wait_ge(s["gp_ready"], g.n + 1)
                wait(pe, s["u0_ready"], g.n * GR)
                for k in range(GR):
                    pe.wait_ge(s["x1_ready"], g.n * GR + k + 1)
                    for c in range(DC):
                        mm = nc.tensor.matmul(ps_zt[:, c, k * N:(k + 1) * N], x1[:, g.par, k, c * P:(c + 1) * P],
                                              gp[:, g.par, k, :], start=True, stop=True)
                mm.then_inc(s["z_done"], 1)

            def w1_product(g):
                pe.wait_ge(s["zt_lo_ready"], g.n + 1)
                for hc in range(HC):
                    if hc == 2:
                        wait(pe, s["f_ready"], g.n)
                    for c in range(DC):
                        mm = split_product(ps[:, W_BANK[hc], :],
                                           (w1_hi[:, c, hc * P:(hc + 1) * P], w1_lo[:, c, hc * P:(hc + 1) * P]),
                                           (zt_hi[:, c, :], zt_lo[:, c, :]), c == 0, c == DC - 1)
                    mm.then_inc(s["w1_done"], 1)

            def w2_product(g, k):
                for hc in range(HC):
                    if k == 0:
                        pe.wait_ge(s["h_lo_ready"], g.n * HC + hc + 1)
                        if hc == 0:
                            pe.wait_ge(s["h_ready"], g.n * HC + 1)
                    if k == 0 and hc == HC - 1:
                        pe.wait_ge(s["h_ready"], g.n * HC + HC)
                    mm = split_product(ps[:, W_BANK[k], 0:W2N],
                                       (h_hi[:, hc, k * N:(k + 1) * N], h_lo[:, hc, k * N:(k + 1) * N]),
                                       (w2_hi[:, hc, :], w2_lo[:, hc, :]), hc == 0, hc == HC - 1)
                mm.then_inc(s["w2_done"], 1)

            def q_transposes(g):
                pe.wait_ge(s["q_ready"], g.n + 1)
                for k in range(GR):
                    mm = nc.tensor.transpose(ps_at[:, k, :], q[:, k * N:(k + 1) * N], ident[:])
                mm.then_inc(s["qt_done"], 1)

            def c2_product(g):
                for k in range(GR):
                    pe.wait_ge(s["u_ready"], g.n * GR + k + 1)
                    mm = nc.tensor.matmul(ps_c2[:, k, :], gp[:, g.par, k, :], u[:, k, :], start=True, stop=True)
                mm.then_inc(s["c2_done"], 1)

            def step(g, n, m, last):
                if g:
                    z_product(g)
                if n:
                    t_product(n)
                if last:
                    c2_product(last)
                if g:
                    w1_product(g)
                if n:
                    s_product(n)
                    p_transposes(n)
                    v_product(n, (0, 1))
                    w_transpose(n)
                    v_product(n, (2, 3))
                if g:
                    w2_product(g, 0)
                if n:
                    p_transpose(n)
                if g:
                    w2_product(g, 1)
                    w2_product(g, 2)
                    if n:
                        pe.wait_ge(s["rr_ready"], n.n + 1)
                    else:
                        pe.wait_ge(s["ssq_ready"], g.n)
                    q_transposes(g)
                    w2_product(g, 3)
                if n:
                    g_product(n)
                if m:
                    transpose_inputs(m)
                    transpose_adj(m)

            first = Group(0, 0)
            wqk_transposes()
            transpose_inputs(first)
            transpose_adj(first)
            m_product()
            pe.wait_ge(s["m_lo_ready"], 1)
            t_product(first)
            w1_transposes()
            s_product(first)
            w2_transposes()
            p_transposes(first)
            pe.wait_ge(s["wv_lo_ready"], 1)
            v_product(first, (0, 1))
            w_transpose(first)
            v_product(first, (2, 3))
            w2_constants()
            p_transpose(first)
            g_product(first)
            transpose_inputs(Group(0, 1))
            transpose_adj(Group(0, 1))
            pe.wait_ge(s["w2_lo_ready"], 1)
            step(Group(0, 0), Group(0, 1), Group(0, 2), None)
            step(Group(0, 1), Group(0, 2), Group(0, 3), Group(0, 0))
            with pe.Fori(1, NG // 2 - 1) as it:
                for k in range(2):
                    step(Group(it, k), Group(it, k + 1), Group(it, k + 2), Group(it - 1, k + 1))
            step(Group(0, NG - 2), Group(0, NG - 1), None, Group(0, NG - 3))
            step(Group(0, NG - 1), None, None, Group(0, NG - 2))
            c2_product(Group(0, NG - 1))

        @block.scalar
        def _(act):
            def zt_high(g):
                act.wait_ge(s["z_done"], g.n + 1)
                nc.scalar.copy(zt_hi[:], ps_zt).then_inc(s["zt_hi_ready"], 1)

            def t_copy(n):
                act.wait_ge(s["t_done"], n.n + 1)
                nc.scalar.copy(tt[:], ps_xt).then_inc(s["tt_ready"], 1)

            def hidden(g):
                for hc in range(HC):
                    act.wait_ge(s["w1_done"], g.n * HC + hc + 1)
                    if hc == 0:
                        wait(act, s["h_lo_ready"], g.n * HC)
                    nc.scalar.activation(h[:, hc, :], ps[:, W_BANK[hc], :], ACT.Relu,
                                         bias=vec_cols[:, hc:hc + 1]).then_inc(s["h_ready"], 1)
                    act.wait_ge(s["h_ready"], g.n * HC + hc + 1)
                    nc.scalar.copy(h_hi[:, hc, :], h[:, hc, :]).then_inc(s["h_hi_ready"], 1)
                wait(act, s["q1_ready"], g.n)
                nc.scalar.activation(sq[:], h[:], ACT.Square).then_inc(s["sq_ready"], 1)

            def final_norm(g):
                act.wait_ge(s["nmr_ready"], g.n + 1)
                wait(act, stored[g.par], 16 * g.half)
                for k in range(GR):
                    nc.scalar.activation(y[:, g.par, k, :], f[:, k, :], ACT.Identity, bias=nmr[:, k:k + 1],
                                         scale=rstd2[:, k:k + 1]).then_inc(s["y_ready"], 1)

            def softmax_exp(n):
                act.wait_ge(s["wbias_ready"], n.n + 1)
                nc.scalar.activation(e_row[:], w_row[:], ACT.Exp, bias=w_bias[:], scale=1.0 / 16.0,
                                     accum_out=e_sum[:]).then_inc(s["e_ready"], 1)

            def u_copy(g):
                for k in range(GR):
                    act.wait_ge(s["w2_done"], g.n * GR + k + 1)
                    if k == 0:
                        wait(act, s["u_ready"], g.n * GR)
                    nc.scalar.copy(u0[:, k, :], ps[:, W_BANK[k], 0:W2N]).then_inc(s["u0_ready"], 1)

            def g_copy(n):
                act.wait_ge(s["g_done"], n.n + 1)
                wait(act, s["c2_done"], n.n - 1)
                nc.scalar.copy(gp[:, n.par], ps_s).then_inc(s["gp_ready"], 1)

            def xt_copy(m):
                for c in range(DC):
                    act.wait_ge(s["xt_done"], m.n * DC + c + 1)
                    nc.scalar.copy(xt[:, c, :], ps_xt[:, c, :]).then_inc(s["xt_ready"], 1)
                for c in range(DC):
                    act.wait_ge(s["xt_ready"], m.n * DC + c + 1)
                    nc.scalar.copy(xt_hi[:, c, :], xt[:, c, :]).then_inc(s["xt_hi_ready"], 1)

            def step(g, n, m, last):
                if g:
                    zt_high(g)
                if n:
                    t_copy(n)
                if g:
                    hidden(g)
                if n:
                    softmax_exp(n)
                if last:
                    final_norm(last)
                if g:
                    u_copy(g)
                if n:
                    g_copy(n)
                if m:
                    xt_copy(m)

            act.dma_start(wqk_raw[:], Wqk.rearrange("(c p) a -> p c a", p=P)).then_inc(s["wqk_loaded"], 16)
            act.dma_start(wv_raw[:], Wv.rearrange("(c p) a -> p c a", p=P)).then_inc(s["wv_loaded"], 16)
            for i, v in enumerate((b1, gamma, beta)):
                act.dma_start(vec_rows[i * HC:(i + 1) * HC], v.rearrange("(c p) -> c p", p=P)).then_inc(
                    s["w12_loaded"], 16)
            act.dma_start(w1_raw[:], W1.rearrange("(c p) a -> p c a", p=P)).then_inc(s["w12_loaded"], 16)
            act.dma_start(w2_raw[:], W2.rearrange("(c p) a -> p c a", p=P)).then_inc(s["w12_loaded"], 16)
            act.dma_start(b2_rows[:], b2.partition_broadcast(P)).then_inc(s["w12_loaded"], 16)
            first = Group(0, 0)
            act.wait_ge(s["setup_tr"], 1)
            nc.scalar.copy(wq_t, ps[:, 4, :].rearrange("p (a d) -> p a d", a=DC)).then_inc(s["setup_copied"], 1)
            xt_copy(first)
            act.wait_ge(s["m_done"], 1)
            nc.scalar.copy(m_hi[:], ps[:, 6, :].rearrange("p (a d) -> p a d", a=DC)).then_inc(s["m_hi_ready"], 1)
            act.wait_ge(s["wv_loaded"], 16)
            nc.scalar.copy(wv_hi[:], wv_raw[:]).then_inc(s["wv_hi_ready"], 1)
            t_copy(first)
            act.wait_ge(s["setup_tr"], 4)
            nc.scalar.copy(w1_hi[:], ps[:, 4:6, :]).then_inc(s["w1_hi_ready"], 1)
            softmax_exp(first)
            act.wait_ge(s["cb_done"], 1)
            nc.scalar.copy(cbeta[:], ps[:, 5, 0:D]).then_inc(s["cbeta_ready"], 1)
            g_copy(first)
            xt_copy(Group(0, 1))
            act.wait_ge(s["consts_ready"], 1)
            act.wait_ge(s["w2c_ready"], 1)
            nc.scalar.copy(w2_hi[:, :, 0:D], w2_c).then_inc(s["w2_hi_ready"], 1)
            step(Group(0, 0), Group(0, 1), Group(0, 2), None)
            step(Group(0, 1), Group(0, 2), Group(0, 3), Group(0, 0))
            with act.Fori(1, NG // 2 - 1) as it:
                for k in range(2):
                    step(Group(it, k), Group(it, k + 1), Group(it, k + 2), Group(it - 1, k + 1))
            step(Group(0, NG - 2), Group(0, NG - 1), None, Group(0, NG - 3))
            step(Group(0, NG - 1), None, None, Group(0, NG - 2))
            final_norm(Group(0, NG - 1))

        @block.vector
        def _(dve):
            V = nc.vector

            def wv_low():
                dve.wait_ge(s["wv_hi_ready"], 1)
                V.tensor_tensor(wv_lo[:], wv_raw[:], wv_hi[:].bitcast(F32), ALU.subtract).then_inc(s["wv_lo_ready"], 1)

            def w1_low():
                dve.wait_ge(s["w1_hi_ready"], 1)
                V.tensor_tensor(w1_lo[:], ps[:, 4:6, :], w1_hi[:].bitcast(F32), ALU.subtract).then_inc(
                    s["w1_lo_ready"], 1)

            def w2_copies():
                dve.wait_ge(s["setup_tr"], 5)
                dve.wait_ge(s["vec_ready"], 1)
                dve.wait_ge(s["consts_ready"], 1)
                for hc in range(HC):
                    V.tensor_scalar(beta_rows[:, hc, :], ones_mean[:], vec_cols[:, 2 * HC + hc:2 * HC + hc + 1],
                                    float(DH), ALU.mult, ALU.mult)
                V.tensor_copy(w2_t, ps[:, 6:8, :].rearrange("p a (b d) -> p (a b) d", d=D)).then_inc(s["w2t_ready"], 1)
                for hc in range(HC):
                    off = (hc % 2) * D
                    ins = V.tensor_scalar(w2_g[:, hc, :], ps[:, 6 + hc // 2, off:off + D],
                                          vec_cols[:, HC + hc:HC + hc + 1], None, ALU.mult)
                ins.then_inc(s["w2g_ready"], 1)

            def w2_centred():
                dve.wait_ge(s["cb_done"], 1)
                dve.wait_ge(s["w2g_ready"], 1)
                V.tensor_tensor(w2_c, w2_g, ps[:, 4, 0:D].unsqueeze(1).to_broadcast([P, HC, D]),
                                ALU.subtract).then_inc(s["w2c_ready"], 1)

            def w2_low():
                dve.wait_ge(s["w2_hi_ready"], 1)
                dve.wait_ge(s["w2c_ready"], 1)
                V.tensor_tensor(w2_lo[:, :, 0:D], w2_c, w2_hi[:, :, 0:D].bitcast(F32),
                                ALU.subtract).then_inc(s["w2_lo_ready"], 1)

            def xt_low(m):
                for c in range(DC):
                    dve.wait_ge(s["xt_hi_ready"], m.n * DC + c + 1)
                    V.tensor_tensor(xt_lo[:, c, :], xt[:, c, :], xt_hi[:, c, :].bitcast(F32),
                                    ALU.subtract).then_inc(s["xt_lo_ready"], 1)

            def final_stats(g):
                dve.wait_ge(s["c2_done"], g.n + 1)
                dve.wait_ge(s["base_ready"], g.n + 1)
                wait(dve, s["y_ready"], g.n * GR)
                V.tensor_tensor(f[:], ps_c2, base[:], ALU.add).then_inc(s["f_ready"], 1)
                dve.wait_ge(s["f_ready"], g.n + 1)
                for k in range(GR):
                    ins = V.bn_stats(st2[:, k, :], f[:, k, :])
                ins.then_inc(s["st2_ready"], 1)
                plain(dve, s["vec_ready"])
                dve.wait_ge(s["st2_ready"], g.n + 1)
                for k in range(GR):
                    ins = V.bn_aggr(mv2[:, k, :], st2[:, k, :])
                ins.then_inc(s["mv2_ready"], 1)
                dve.wait_ge(s["mv2_ready"], g.n + 1)
                V.tensor_scalar(ve2[:], mv2[:, :, 1], EPS, None, ALU.add).then_inc(s["ve2_ready"], 1)

            def final_bias(g):
                dve.wait_ge(s["rstd2_ready"], g.n + 1)
                V.scalar_tensor_tensor(out=nmr[:], in0=mv2[:, :, 0], scalar=-1.0, in1=rstd2[:], op0=ALU.mult,
                                       op1=ALU.mult).then_inc(s["nmr_ready"], 1)

            def zt_low(g):
                dve.wait_ge(s["zt_hi_ready"], g.n + 1)
                V.tensor_tensor(zt_lo[:], ps_zt, zt_hi[:].bitcast(F32), ALU.subtract).then_inc(s["zt_lo_ready"], 1)

            def incidence(n):
                dve.wait_ge(loaded[n.par], 16 * LOADS * (n.half + 1))
                wait(dve, s["pn_ready"], n.n)
                V.tensor_scalar(hn[:], a_in[:, n.par], 0.0, None, ALU.not_equal).then_inc(s["hn_ready"], 1)
                dve.wait_ge(s["at_done"], n.n + 1)
                wait(dve, s["g_done"], n.n)
                V.tensor_scalar(ht[:], ps_at, 0.0, None, ALU.not_equal).then_inc(s["ht_ready"], 1)
                dve.wait_ge(s["ht_ready"], n.n + 1)
                V.tensor_reduce(cnt[:], ht[:], AX_X, ALU.add).then_inc(s["cnt_ready"], 1)
                dve.wait_ge(s["cnt_ready"], n.n + 1)
                V.tensor_scalar(cnt1[:], cnt[:], 1.0, None, ALU.max).then_inc(s["cnt1_ready"], 1)
                dve.wait_ge(s["cnt1_ready"], n.n + 1)
                V.reciprocal(be[:], cnt1[:]).then_inc(s["be_ready"], 1)

            def degrees(n):
                dve.wait_ge(s["he_ready"], n.n + 1)
                V.tensor_reduce(deg[:], he[:], AX_X, ALU.add).then_inc(s["deg_ready"], 1)
                dve.wait_ge(s["deg_ready"], n.n + 1)
                V.scalar_tensor_tensor(out=deg1[:], in0=deg[:], scalar=0.0, in1=deg[:], op0=ALU.is_le,
                                       op1=ALU.max).then_inc(s["deg1_ready"], 1)
                dve.wait_ge(s["deg1_ready"], n.n + 1)
                V.reciprocal(deg_inv[:], deg1[:]).then_inc(s["dinv_ready"], 1)
                dve.wait_ge(s["dinv_ready"], n.n + 1)
                V.scalar_tensor_tensor(out=dn[:], in0=deg[:], scalar=0.0, in1=deg_inv[:], op0=ALU.is_gt,
                                       op1=ALU.mult).then_inc(s["dn_ready"], 1)

            def hidden_low(g, hc):
                dve.wait_ge(s["h_hi_ready"], g.n * HC + hc + 1)
                V.tensor_tensor(h_lo[:, hc, :], h[:, hc, :], h_hi[:, hc, :].bitcast(F32),
                                ALU.subtract).then_inc(s["h_lo_ready"], 1)

            def dots(n):
                dve.wait_ge(s["am_ready"], n.n + 1)
                dve.wait_ge(s["s_done"], n.n + 1)
                for k in range(GR):
                    V.tensor_tensor_reduce(dot_junk[:, k, :], ps_s[:, k, :], am[:, k, :], 1.0, 0.0, ALU.mult, ALU.add,
                                           w_col[:, k:k + 1]).then_inc(s["w_ready"], 1)

            def r_scale(n):
                dve.wait_ge(s["pt_done"], n.n + 1)
                dve.wait_ge(s["be_ready"], n.n + 1)
                V.tensor_tensor(rr[:], ps_at, be[:].unsqueeze(2).to_broadcast([P, GR, N]),
                                ALU.mult).then_inc(s["rr_ready"], 1)

            def softmax_max(n):
                dve.wait_ge(s["wt_done"], n.n + 1)
                V.tensor_tensor(w_row[:], ps[0:GR, 2, 0:N], mrow_in[:, n.par], ALU.mult).then_inc(s["wrow_ready"], 1)
                dve.wait_ge(s["wrow_ready"], n.n + 1)
                V.tensor_reduce(w_max[:], w_row[:], AX_X, ALU.max).then_inc(s["wmax_ready"], 1)
                dve.wait_ge(s["wmax_ready"], n.n + 1)
                V.tensor_scalar(w_bias[:], w_max[:], -1.0 / 16.0, None, ALU.mult).then_inc(s["wbias_ready"], 1)

            def softmax_scale(n):
                dve.wait_ge(s["e_ready"], n.n + 1)
                V.reciprocal(e_inv[:], e_sum[:]).then_inc(s["einv_ready"], 1)
                dve.wait_ge(s["einv_ready"], n.n + 1)
                V.tensor_scalar(p_row[:], e_row[:], e_inv[:], None, ALU.mult).then_inc(s["prow_ready"], 1)

            def residual(n):
                dve.wait_ge(s["pcol_done"], n.n + 1)
                V.tensor_copy(p_col[:], ps[:, 2, N:N + GR]).then_inc(s["pcol_ready"], 1)
                dve.wait_ge(s["pcol_ready"], n.n + 1)
                for k in range(GR):
                    dve.wait_ge(s["v_done"], n.n * GR + k + 1)
                    V.scalar_tensor_tensor(out=r1[:, k, :], in0=ps_v[:, k, :], scalar=p_col[:, k:k + 1],
                                           in1=x_in[:, n.par, k, :], op0=ALU.mult,
                                           op1=ALU.add).then_inc(s["r1_ready"], 1)

            def x1_stats(n):
                for k in range(GR):
                    dve.wait_ge(s["r1_ready"], n.n * GR + k + 1)
                    V.bn_stats(st1[:, k, :], r1[:, k, :]).then_inc(s["st1_ready"], 1)

            def x1_aggregate(n):
                plain(dve, s["vec_ready"])
                dve.wait_ge(s["st1_ready"], n.n * GR + GR)
                for k in range(GR):
                    ins = V.bn_aggr(mv1[:, k, :], st1[:, k, :])
                ins.then_inc(s["mv1_ready"], 1)
                dve.wait_ge(s["mv1_ready"], n.n + 1)
                V.tensor_scalar(ve1[:], mv1[:, :, 1], EPS, None, ALU.add).then_inc(s["ve1_ready"], 1)

            def x1_apply(n):
                dve.wait_ge(s["rstd1_ready"], n.n + 1)
                wait(dve, s["base_ready"], n.n - 1)
                for k in range(GR):
                    V.tensor_scalar(x1[:, n.par, k, :], r1[:, k, :], mv1[:, k, 0:1], rstd1[:, k:k + 1],
                                    ALU.subtract, ALU.mult).then_inc(s["x1_ready"], 1)

            def square_sums(g):
                dve.wait_ge(s["qt_done"], g.n + 1)
                V.tensor_reduce(ssq[:], ps_at, AX_X, ALU.add).then_inc(s["ssq_ready"], 1)

            def hidden_stats(g):
                dve.wait_ge(s["u0_ready"], g.n * GR + GR)
                V.scalar_tensor_tensor(out=hmu2[:], in0=u0[:, :, D], scalar=-1.0, in1=u0[:, :, D],
                                       op0=ALU.mult, op1=ALU.mult).then_inc(s["hmu2_ready"], 1)
                dve.wait_ge(s["hmu2_ready"], g.n + 1)
                V.scalar_tensor_tensor(out=hvar[:], in0=ssq[:], scalar=1.0 / DH, in1=hmu2[:], op0=ALU.mult,
                                       op1=ALU.add).then_inc(s["hvar_ready"], 1)
                dve.wait_ge(s["hvar_ready"], g.n + 1)
                V.tensor_scalar(hve[:], hvar[:], 0.0, EPS, ALU.max, ALU.add).then_inc(s["hve_ready"], 1)

            def u_rows(g):
                dve.wait_ge(s["rs_ready"], g.n + 1)
                wait(dve, s["c2_done"], g.n)
                for k in range(GR):
                    V.scalar_tensor_tensor(out=u[:, k, :], in0=u0[:, k, 0:D], scalar=rs[:, k:k + 1], in1=cbeta[:],
                                           op0=ALU.mult, op1=ALU.add).then_inc(s["u_ready"], 1)

            def step(g, n, m, last):
                if g:
                    zt_low(g)
                if n:
                    incidence(n)
                if last:
                    final_stats(last)
                if g:
                    hidden_low(g, 0)
                if n:
                    degrees(n)
                if g:
                    for hc in range(1, HC):
                        hidden_low(g, hc)
                if last:
                    final_bias(last)
                if n:
                    dots(n)
                    r_scale(n)
                    softmax_max(n)
                    softmax_scale(n)
                    residual(n)
                    x1_stats(n)
                    x1_aggregate(n)
                if g:
                    square_sums(g)
                if n:
                    x1_apply(n)
                if g:
                    hidden_stats(g)
                if m:
                    xt_low(m)
                if g:
                    u_rows(g)

            first = Group(0, 0)
            dve.wait_ge(s["setup_tr"], 2)
            V.tensor_copy(wk_t, ps[:, 5, :].rearrange("p (a d) -> p a d", a=DC)).then_inc(s["setup_copied"], 1)
            xt_low(first)
            dve.wait_ge(s["m_hi_ready"], 1)
            V.tensor_tensor(m_lo[:], ps[:, 6, :].rearrange("p (a d) -> p a d", a=DC), m_hi[:].bitcast(F32),
                            ALU.subtract).then_inc(s["m_lo_ready"], 1)
            incidence(first)
            wv_low()
            dve.wait_ge(s["setup_tr"], 3)
            V.tensor_copy(vec_cols[:], ps[:, 7, 0:3 * HC]).then_inc(s["vec_ready"], 1)
            degrees(first)
            w1_low()
            dots(first)
            r_scale(first)
            softmax_max(first)
            w2_copies()
            softmax_scale(first)
            residual(first)
            x1_stats(first)
            x1_aggregate(first)
            w2_centred()
            x1_apply(first)
            xt_low(Group(0, 1))
            w2_low()
            dve.wait_ge(s["cbeta_ready"], 1)
            step(Group(0, 0), Group(0, 1), Group(0, 2), None)
            step(Group(0, 1), Group(0, 2), Group(0, 3), Group(0, 0))
            with dve.Fori(1, NG // 2 - 1) as it:
                for k in range(2):
                    step(Group(it, k), Group(it, k + 1), Group(it, k + 2), Group(it - 1, k + 1))
            step(Group(0, NG - 2), Group(0, NG - 1), None, Group(0, NG - 3))
            step(Group(0, NG - 1), None, None, Group(0, NG - 2))
            final_stats(Group(0, NG - 1))
            final_bias(Group(0, NG - 1))

        @block.gpsimd
        def _(pool):
            Q = nc.gpsimd

            def setup():
                Q.memset(ident[:], 0.0).then_inc(s["ident_zero"], 1)
                pool.wait_ge(s["ident_zero"], 1)
                Q.affine_select(out=ident[:], in_=ident[:], compare_op=ALU.not_equal, fill=1.0, base=0,
                                pattern=[[-1, P]], channel_multiplier=1).then_inc(s["ident_ready"], 1)
                Q.memset(neg_half[:], -0.5)
                Q.memset(w2_hi[:, :, D:W2N].bitcast(F32), 1.0 / DH)
                Q.memset(w2_lo[:, :, D:W2N].bitcast(F32), 0.0)
                Q.memset(ones_mean[:], 1.0 / DH).then_inc(s["consts_ready"], 1)
                pool.wait_ge(s["consts_ready"], 1)

            def masked_adj(n):
                pool.wait_ge(loaded[n.par], 16 * LOADS * (n.half + 1))
                wait(pool, s["w_ready"], n.n * GR)
                Q.tensor_tensor(am[:], a_in[:, n.par], mask_in[:, n.par], ALU.mult).then_inc(s["am_ready"], 1)

            def base_rows(g):
                pool.wait_ge(s["x1_ready"], g.n * GR + GR)
                Q.tensor_tensor(base0[:], x1[:, g.par], b2_rows[:].unsqueeze(1).to_broadcast([P, GR, D]),
                                ALU.add).then_inc(s["base0_ready"], 1)
                pool.wait_ge(s["base0_ready"], g.n + 1)
                wait(pool, s["f_ready"], g.n)
                Q.tensor_tensor(base[:], base0[:], x1[:, g.par], ALU.add).then_inc(s["base_ready"], 1)

            def final_rstd(g):
                pool.wait_ge(s["ve2_ready"], g.n + 1)
                wait(pool, s["y_ready"], g.n * GR)
                Q.tensor_tensor(rstd2[:], ve2[:], neg_half[:], ALU.pow).then_inc(s["rstd2_ready"], 1)

            def edge_weights(n):
                pool.wait_ge(s["hn_ready"], n.n + 1)
                wait(pool, s["deg_ready"], n.n)
                Q.tensor_tensor(he[:], hn[:], edge_in[:, n.par], ALU.mult).then_inc(s["he_ready"], 1)

            def scaled_incidence(n):
                pool.wait_ge(s["dn_ready"], n.n + 1)
                wait(pool, s["pt_done"], n.n)
                Q.tensor_tensor(pn[:], hn[:], dn[:].unsqueeze(2).to_broadcast([P, GR, N]),
                                ALU.mult).then_inc(s["pn_ready"], 1)

            def square_blocks(g):
                pool.wait_ge(s["sq_ready"], g.n + 1)
                Q.tensor_tensor(q1[:], sq[:, 0:2, :], sq[:, 2:4, :], ALU.add).then_inc(s["q1_ready"], 1)
                pool.wait_ge(s["q1_ready"], g.n + 1)
                wait(pool, s["qt_done"], g.n)
                Q.tensor_tensor(q[:], q1[:, 0, :], q1[:, 1, :], ALU.add).then_inc(s["q_ready"], 1)

            def hidden_rstd(g):
                pool.wait_ge(s["hve_ready"], g.n + 1)
                wait(pool, s["u_ready"], g.n * GR)
                Q.tensor_tensor(rs[:], hve[:], neg_half[:], ALU.pow).then_inc(s["rs_ready"], 1)

            def x1_rstd(n):
                pool.wait_ge(s["ve1_ready"], n.n + 1)
                Q.tensor_tensor(rstd1[:], ve1[:], neg_half[:], ALU.pow).then_inc(s["rstd1_ready"], 1)

            def step(g, n, last):
                if n:
                    masked_adj(n)
                    edge_weights(n)
                    scaled_incidence(n)
                if last:
                    final_rstd(last)
                if g:
                    square_blocks(g)
                if n:
                    x1_rstd(n)
                if g:
                    hidden_rstd(g)
                    base_rows(g)

            setup()
            step(None, Group(0, 0), None)
            pool.wait_ge(s["w12_loaded"], 16 * 6)
            step(Group(0, 0), Group(0, 1), None)
            step(Group(0, 1), Group(0, 2), Group(0, 0))
            with pool.Fori(1, NG // 2 - 1) as it:
                for k in range(2):
                    step(Group(it, k), Group(it, k + 1), Group(it - 1, k + 1))
            step(Group(0, NG - 2), Group(0, NG - 1), Group(0, NG - 3))
            step(Group(0, NG - 1), None, Group(0, NG - 2))
            final_rstd(Group(0, NG - 1))


_INS = ['x', 'adj', 'nodemask', 'L0_gnn_Wqk', 'L0_gnn_Wv', 'L1_gnn_W1', 'L1_gnn_b1', 'L1_gnn_gamma', 'L1_gnn_beta',
        'L1_gnn_W2', 'L1_gnn_b2']


def kernel(**inputs):
    import numpy as _np
    import concourse.bacc as _bacc
    from concourse import mybir as _mybir
    from concourse.bass_utils import run_bass_kernel_spmd as _run

    nc = _bacc.Bacc("TRN2", target_bir_lowering=False, num_devices=1)
    arrays, args = {}, []
    for name in _INS:
        a = _np.ascontiguousarray(inputs[name])
        arrays[f"in_{name}"] = a
        args.append(nc.dram_tensor(f"in_{name}", a.shape, _mybir.dt.from_np(a.dtype), kind="ExternalInput").ap())
    shape = inputs['x'].shape
    args.append(nc.dram_tensor("out_x", shape, _mybir.dt.float32, kind="ExternalOutput").ap())
    build_program(nc, *args)
    r = _run(nc, [arrays], core_ids=[0])
    return r.results[0]["out_x"]
```

```python
from contextlib import ExitStack

import concourse.bass as bass
from concourse import mybir

ALU = mybir.AluOpType
ACT = mybir.ActivationFunctionType
F32 = mybir.dt.float32
F32R = mybir.dt.float32r
BF16 = mybir.dt.bfloat16
AX_X = mybir.AxisListType.X
P = 128
EPS = 1e-5


class Group:

    def __init__(self, it, k):
        self.n = it * 2 + k
        self.half = it + k // 2
        self.par = k % 2


def wait(eng, sem, value):
    if isinstance(value, int) and value <= 0:
        return
    eng.wait_ge(sem, value)


def plain(eng, sem):
    eng.wait_ge(sem, 1)


def build_program(nc, x, adj, nodemask, Wqk, Wv, W1, b1, gamma, beta, W2, b2, out):
    B, N, D = x.shape
    DH = W1.shape[0]
    GR = 4
    NG = B // GR
    DC = D // P
    HC = DH // P
    GN = GR * N
    W2N = D + 2
    ALL = (0, 1, 2, 3)
    HALVES = ((0, 1), (2, 3))
    assert N == P and DC == 2 and HC == 4 and GN == 512 and NG % 2 == 0

    with ExitStack() as ctx:
        def sb(name, shape, dt=F32):
            return ctx.enter_context(nc.sbuf_tensor(name, shape, dt))

        def sem(name):
            return ctx.enter_context(nc.semaphore(name))

        ident = sb("ident", [P, P])
        ident_bf = sb("ident_bf", [P, P], BF16)
        neg_half = sb("neg_half", [P, GR])
        ones_mean = sb("ones_mean", [P, P])
        ones = sb("ones", [P, P])
        b2_rows = sb("b2_rows", [P, D])
        cbeta = sb("cbeta", [P, D])
        vec_rows = sb("vec_rows", [3 * HC, P])
        vec_cols = sb("vec_cols", [P, 3 * HC])
        m_hi, m_lo = sb("m_hi", [P, DC, D], F32R), sb("m_lo", [P, DC, D], F32R)
        wv_hi, wv_lo = sb("wv_hi", [P, DC, D], F32R), sb("wv_lo", [P, DC, D], F32R)
        w1_hi, w1_lo = sb("w1_hi", [P, DC, DH], F32R), sb("w1_lo", [P, DC, DH], F32R)
        w2_hi, w2_lo = sb("w2_hi", [P, HC, W2N], F32R), sb("w2_lo", [P, HC, W2N], F32R)

        x_in = sb("x_in", [P, 2, GR, D])
        a_in = sb("a_in", [P, 2, GR, N])
        mask_in = sb("mask_in", [P, 2, GR, N])
        edge_in = sb("edge_in", [P, 2, GR, N])
        mrow_in = sb("mrow_in", [GR, 2, N])
        xt = sb("xt", [P, DC, GN])
        xt_hi, xt_lo = sb("xt_hi", [P, DC, GN], F32R), sb("xt_lo", [P, DC, GN], F32R)
        tt = sb("tt", [P, DC, GN])
        am = sb("am", [P, GR, N])
        dot_junk = sb("dot_junk", [P, GR, N])
        w_col = sb("w_col", [P, GR])
        w_row = sb("w_row", [GR, N])
        w_max = sb("w_max", [GR, 1])
        w_bias = sb("w_bias", [GR, 1])
        e_row = sb("e_row", [GR, N])
        e_sum = sb("e_sum", [GR, 1])
        e_inv = sb("e_inv", [GR, 1])
        p_row = sb("p_row", [GR, N])
        p_col = sb("p_col", [P, GR])
        hn = sb("hn", [P, GR, N], BF16)
        ht = sb("ht", [P, GR, N])
        he = sb("he", [P, GR, N])
        rr = sb("rr", [P, GR, N])
        cnt = sb("cnt", [P, GR])
        cnt1 = sb("cnt1", [P, GR])
        be = sb("be", [P, GR])
        deg = sb("deg", [P, GR])
        deg1 = sb("deg1", [P, GR])
        deg_inv = sb("deg_inv", [P, GR])
        dn = sb("dn", [P, GR])
        dn_rows = sb("dn_rows", [P, N, GR])
        dn_dram = nc.dram_tensor("dn_dram", (NG, P, GR), F32).ap()
        gp = sb("gp", [P, 2, GR, N])
        gp_hi, gp_lo = sb("gp_hi", [P, 2, GR, N], F32R), sb("gp_lo", [P, 2, GR, N], F32R)
        r1 = sb("r1", [P, GR, D])
        st1 = sb("st1", [P, GR, 6])
        mv1 = sb("mv1", [P, GR, 2])
        ve1 = sb("ve1", [P, GR])
        rstd1 = sb("rstd1", [P, GR])
        x1 = sb("x1", [P, 2, GR, D])
        zt_hi, zt_lo = sb("zt_hi", [P, DC, GN], F32R), sb("zt_lo", [P, DC, GN], F32R)
        h = sb("h", [P, HC, GN])
        h_hi, h_lo = sb("h_hi", [P, HC, GN], F32R), sb("h_lo", [P, HC, GN], F32R)
        sq = sb("sq", [P, HC, GN])
        q1 = sb("q1", [P, 2, GN])
        q = sb("q", [P, GN])
        ssq = sb("ssq", [P, GR])
        hmu2 = sb("hmu2", [P, GR])
        hvar = sb("hvar", [P, GR])
        hve = sb("hve", [P, GR])
        rs = sb("rs", [P, GR])
        u0 = sb("u0", [P, GR, W2N])
        u = sb("u", [P, GR, D])
        u_hi, u_lo = sb("u_hi", [P, GR, D], F32R), sb("u_lo", [P, GR, D], F32R)
        base0 = sb("base0", [P, GR, D])
        base = sb("base", [P, GR, D])
        f = sb("f", [P, 2, GR, D])
        st2 = sb("st2", [P, GR, 6])
        mv2 = sb("mv2", [P, GR, 2])
        ve2 = sb("ve2", [P, GR])
        rstd2 = sb("rstd2", [P, GR])
        nmr = sb("nmr", [P, GR])
        y = sb("y", [P, 2, GR, D])

        wqk_raw = sb("wqk_raw", [P, DC, 2 * D])
        wv_raw = sb("wv_raw", [P, DC, D])
        w1_raw = sb("w1_raw", [P, HC, D])
        w2_raw = sb("w2_raw", [P, DC, DH])
        wq_t = h[:, 0, :].rearrange("p (a d) -> p a d", a=DC)
        wk_t = h[:, 1, :].rearrange("p (a d) -> p a d", a=DC)
        w2_t = sq[:, 0:2, :].rearrange("p a (b d) -> p (a b) d", d=D)
        w2_g = sq[:, 2:4, :].rearrange("p a (b d) -> p (a b) d", d=D)
        w2_c = u
        beta_rows = f[:, 0, 0:2, :].rearrange("p a (b d) -> p (a b) d", d=P)

        ps = ctx.enter_context(nc.psum_tensor("ps", [P, 8, 512], F32))
        ps_xt = ps[:, 0:2, :]
        ps_v = ps[:, 0:2, :].rearrange("p a (b d) -> p (a b) d", d=D)
        ps_s = ps[:, 2, :].rearrange("p (g n) -> p g n", g=GR)
        ps_g = ps[:, 3, :].rearrange("p (g n) -> p g n", g=GR)
        ps_ht = ps[:, 3, 0:GN // 2].bitcast(BF16).rearrange("p (g n) -> p g n", g=GR)
        ps_qt = ps_g
        ps_zt = ps[:, 4:6, :]
        W1_BANK = (4, 5, 6, 7)
        W2_BANK = (4, 5, 4, 2)
        LAST_BANK = (2, 3, 4, 5)
        ps_last_qt = ps[:, 7, :].rearrange("p (g n) -> p g n", g=GR)
        ps_c2 = ps[:, 6:8, :].rearrange("p a (b d) -> p (a b) d", d=D)

        s = {name: sem(name) for name in """
            wqk_loaded wv_loaded w1_loaded vec_loaded w2_loaded b2_loaded ident_zero ident_ready ones_ready
            consts_ready wqk_tr wqk_copied m_done vec_tr w1_tr w2_tr
            m_hi_ready m_lo_ready wv_hi_ready wv_lo_ready w1_hi_ready w1_lo_ready w2_hi_ready w2_lo_ready
            vec_ready beta_ready w2t_ready w2g_ready w2mean_done w2beta_done w2c_ready cbeta_ready
            xt_done ht_done t_done s_done v_done wt_done pcol_done g_done z_done w1_done w2_done qt_done c2_done
            xt_ready xt_hi_ready xt_lo_ready tt_ready am_ready w_ready wrow_ready wmax_ready wbias_ready e_ready
            einv_ready prow_ready pcol_ready
            hn_ready ht_ready cnt_ready cnt1_ready be_ready he_ready deg_ready deg1_ready
            dinv_ready dn_ready dn_stored dn_rows_loaded
            rr_ready gp_ready gp_hi_ready gp_lo_ready r1_ready st1_ready mv1_ready ve1_ready rstd1_ready x1_ready
            zt_hi_ready zt_lo_ready h_ready h_hi_ready h_lo0_ready h_lo_ready sq_ready q1_ready q_ready ssq_ready
            hmu2_ready hvar_ready hve_ready rs_ready u0_ready u_ready u_hi_ready u_lo_ready
            base0_ready base_ready f_ready st2_ready mv2_ready ve2_ready rstd2_ready nmr_ready y_ready y2_ready
            """.split()}
        x_loaded = [sem("x_loaded_even"), sem("x_loaded_odd")]
        a_loaded = [sem("a_loaded_even"), sem("a_loaded_odd")]
        m_loaded = [sem("m_loaded_even"), sem("m_loaded_odd")]
        stored = [sem("stored_even"), sem("stored_odd")]
        M_LOADS = 3

        block = ctx.enter_context(nc.Block())

        @block.sync
        def _(sp):
            def load(g):
                rows = bass.ds(g.n * GR, GR)
                sp.dma_start(x_in[:, g.par], x[rows].rearrange("b n d -> n b d")).then_inc(x_loaded[g.par], 16)
                sp.dma_start(a_in[:, g.par], adj[rows].rearrange("b n e -> n b e")).then_inc(a_loaded[g.par], 16)
                sp.dma_start(edge_in[:, g.par], adj[rows, 0, :].partition_broadcast(P)).then_inc(m_loaded[g.par], 16)
                sp.dma_start(mask_in[:, g.par], nodemask[rows].partition_broadcast(P)).then_inc(m_loaded[g.par], 16)
                sp.dma_start(mrow_in[:, g.par], nodemask[rows]).then_inc(m_loaded[g.par], 16)

            def load_over(old, new):
                wait(sp, s["mv1_ready"], old.n + 1)
                wait(sp, s["am_ready"], old.n + 1)
                load(new)

            def spread_dn(n):
                plain(sp, a_loaded[0])
                sp.wait_ge(s["dn_ready"], n.n + 1)
                sp.dma_start(dn_dram[bass.ds(n.n, 1)].rearrange("o p g -> p (o g)"), dn[:]).then_inc(
                    s["dn_stored"], 16)
                sp.wait_ge(s["dn_stored"], 16 * (n.n + 1))
                wait(sp, s["gp_ready"], n.n)
                sp.dma_start(dn_rows[:], dn_dram[bass.ds(n.n, 1)].rearrange("o p g -> o (p g)").partition_broadcast(
                    P)).then_inc(s["dn_rows_loaded"], 16)

            def store(g):
                plain(sp, a_loaded[0])
                sp.wait_ge(s["y_ready"], g.n * GR + GR)
                sp.dma_start(out[bass.ds(g.n * GR, GR)].rearrange("b n d -> n b d"), y[:, g.par]).then_inc(
                    stored[g.par], 16)

            def store_half(g, ks, sem, count):
                sp.wait_ge(sem, count)
                sp.dma_start(out[g.n * GR + ks[0]:g.n * GR + ks[-1] + 1].rearrange("b n d -> n b d"),
                             y[:, g.par, ks[0]:ks[-1] + 1]).then_inc(stored[g.par], 16)

            rows = bass.ds(0, GR)
            sp.dma_start(x_in[:, 0], x[rows].rearrange("b n d -> n b d")).then_inc(x_loaded[0], 16)
            sp.dma_start(a_in[:, 0], adj[rows].rearrange("b n e -> n b e")).then_inc(a_loaded[0], 16)
            sp.dma_start(w1_raw[:], W1.rearrange("(c p) a -> p c a", p=P)).then_inc(s["w1_loaded"], 16)
            sp.dma_start(edge_in[:, 0], adj[rows, 0, :].partition_broadcast(P)).then_inc(m_loaded[0], 16)
            sp.dma_start(mask_in[:, 0], nodemask[rows].partition_broadcast(P)).then_inc(m_loaded[0], 16)
            sp.dma_start(mrow_in[:, 0], nodemask[rows]).then_inc(m_loaded[0], 16)
            for i, v in enumerate((b1, gamma, beta)):
                sp.dma_start(vec_rows[i * HC:(i + 1) * HC], v.rearrange("(c p) -> c p", p=P)).then_inc(
                    s["vec_loaded"], 16)
            sp.dma_start(w2_raw[:], W2.rearrange("(c p) a -> p c a", p=P)).then_inc(s["w2_loaded"], 16)
            load(Group(0, 1))
            sp.dma_start(b2_rows[:], b2.partition_broadcast(P)).then_inc(s["b2_loaded"], 16)
            spread_dn(Group(0, 0))
            for k in range(2):
                load_over(Group(0, k), Group(0, k + 2))
                spread_dn(Group(0, k + 1))
            with sp.Fori(1, NG // 2 - 1) as it:
                for k in range(2):
                    load_over(Group(it, k), Group(it, k + 2))
                    spread_dn(Group(it, k + 1))
                    store(Group(it - 1, k))
            spread_dn(Group(0, NG - 1))
            for k in range(NG - 4, NG - 1):
                store(Group(0, k))
            store_half(Group(0, NG - 1), HALVES[0], s["y_ready"], (NG - 1) * GR + 2)
            store_half(Group(0, NG - 1), HALVES[1], s["y2_ready"], 2)
            sp.wait_ge(stored[0], 16 * (NG // 2))
            sp.wait_ge(stored[1], 16 * (NG // 2 + len(HALVES) - 1))

        @block.tensor
        def _(pe):
            def split_product(o, w, m, first, last):
                for j, (a, b) in enumerate(((1, 0), (0, 1), (0, 0))):
                    mm = nc.tensor.matmul(o, w[a], m[b], start=first and j == 0, stop=last and j == 2)
                return mm

            def warm_up():
                pe.wait_ge(s["ident_ready"], 1)
                for i in range(12):
                    nc.tensor.transpose(ps[:, 7, (i % 4) * P:(i % 4 + 1) * P], ident[:], ident[:])

            def wqk_transposes():
                pe.wait_ge(s["wqk_loaded"], 16)
                for part in range(2):
                    for a in range(DC):
                        for c in range(DC):
                            mm = nc.tensor.transpose(ps[:, 4 + part, a * D + c * P:a * D + (c + 1) * P],
                                                     wqk_raw[:, c, part * D + a * P:part * D + (a + 1) * P], ident[:])
                    mm.then_inc(s["wqk_tr"], 1)

            def m_product():
                pe.wait_ge(s["wqk_copied"], 2)
                for c in range(DC):
                    for a in range(DC):
                        mm = nc.tensor.matmul(ps[:, 6, c * D:(c + 1) * D], wq_t[:, a, c * P:(c + 1) * P],
                                              wk_t[:, a, :], start=a == 0, stop=a == DC - 1)
                mm.then_inc(s["m_done"], 1)

            def w1_transposes():
                pe.wait_ge(s["w1_loaded"], 16)
                for c in range(DC):
                    for hc in range(HC):
                        mm = nc.tensor.transpose(ps[:, 4 + c, hc * P:(hc + 1) * P],
                                                 w1_raw[:, hc, c * P:(c + 1) * P], ident[:])
                mm.then_inc(s["w1_tr"], 1)
                pe.wait_ge(s["vec_loaded"], 16 * 3)
                nc.tensor.transpose(ps[:, 7, 0:3 * HC], vec_rows[:], ident[0:3 * HC, 0:3 * HC]).then_inc(
                    s["vec_tr"], 1)

            def w2_transposes():
                pe.wait_ge(s["w2_loaded"], 16)
                pe.wait_ge(s["vec_ready"], 1)
                for hc in range(HC):
                    for c in range(DC):
                        off = (hc % 2) * D + c * P
                        mm = nc.tensor.transpose(ps[:, 6 + hc // 2, off:off + P],
                                                 w2_raw[:, c, hc * P:(hc + 1) * P], ident[:])
                mm.then_inc(s["w2_tr"], 1)

            def w2_mean():
                pe.wait_ge(s["w1_lo_ready"], 1)
                pe.wait_ge(s["w2g_ready"], 1)
                for hc in range(HC):
                    mm = nc.tensor.matmul(ps[:, 4, 0:D], ones_mean[:], w2_g[:, hc, :], start=hc == 0,
                                          stop=hc == HC - 1)
                mm.then_inc(s["w2mean_done"], 1)

            def w2_beta():
                pe.wait_ge(s["w2t_ready"], 1)
                pe.wait_ge(s["beta_ready"], 1)
                for hc in range(HC):
                    mm = nc.tensor.matmul(ps[:, 5, 0:D], beta_rows[:, hc, :], w2_t[:, hc, :],
                                          start=hc == 0, stop=hc == HC - 1)
                mm.then_inc(s["w2beta_done"], 1)

            def transpose_inputs(m):
                pe.wait_ge(x_loaded[m.par], 16 * (m.half + 1))
                wait(pe, s["r1_ready"], m.n * GR)
                for c in range(DC):
                    for k in range(GR):
                        mm = nc.tensor.transpose(ps_xt[:, c, k * N:(k + 1) * N],
                                                 x_in[:, m.par, k, c * P:(c + 1) * P], ident[:])
                    mm.then_inc(s["xt_done"], 1)

            def transpose_incidence(m):
                pe.wait_ge(s["hn_ready"], m.n + 1)
                wait(pe, s["gp_ready"], m.n)
                wait(pe, s["ssq_ready"], m.n - 1)
                for k in range(GR):
                    mm = nc.tensor.transpose(ps_ht[:, k, :], hn[:, k, :], ident_bf[:])
                mm.then_inc(s["ht_done"], 1)

            def t_product(n):
                pe.wait_ge(s["xt_ready"], n.n * DC + DC)
                for c in range(DC):
                    pe.wait_ge(s["xt_lo_ready"], n.n * DC + c + 1)
                    for co in range(DC):
                        mm = split_product(ps_xt[:, co, :],
                                           (m_hi[:, c, co * P:(co + 1) * P], m_lo[:, c, co * P:(co + 1) * P]),
                                           (xt_hi[:, c, :], xt_lo[:, c, :]), c == 0, c == DC - 1)
                mm.then_inc(s["t_done"], 1)

            def s_product(n):
                pe.wait_ge(s["tt_ready"], n.n + 1)
                pe.wait_ge(s["xt_ready"], n.n * DC + DC)
                wait(pe, s["u0_ready"], n.n * GR - GR)
                for k in range(GR):
                    for c in range(DC):
                        mm = nc.tensor.matmul(ps_s[:, k, :], tt[:, c, k * N:(k + 1) * N], xt[:, c, k * N:(k + 1) * N],
                                              start=c == 0, stop=c == DC - 1)
                mm.then_inc(s["s_done"], 1)

            def g_product(n):
                pe.wait_ge(s["rr_ready"], n.n + 1)
                for k in range(GR):
                    mm = nc.tensor.matmul(ps_g[:, k, :], ht[:, k, :], rr[:, k, :], start=True, stop=True)
                mm.then_inc(s["g_done"], 1)

            def v_product(n, ks):
                for k in ks:
                    for c in range(DC):
                        mm = split_product(ps_v[:, k, :], (xt_hi[:, c, k * N:(k + 1) * N],
                                                           xt_lo[:, c, k * N:(k + 1) * N]),
                                           (wv_hi[:, c, :], wv_lo[:, c, :]), c == 0, c == DC - 1)
                    mm.then_inc(s["v_done"], 1)

            def w_transpose(n):
                pe.wait_ge(s["w_ready"], n.n * GR + GR)
                nc.tensor.transpose(ps[0:GR, 2, 0:N], w_col[:], ident[:]).then_inc(s["wt_done"], 1)

            def p_transpose(n):
                plain(pe, s["ident_ready"])
                pe.wait_ge(s["prow_ready"], n.n + 1)
                nc.tensor.transpose(ps[:, 2, N:N + GR], p_row[:], ident[0:GR, 0:GR]).then_inc(s["pcol_done"], 1)

            def z_product(g):
                pe.wait_ge(s["gp_ready"], g.n + 1)
                wait(pe, s["u0_ready"], g.n * GR - 1)
                for k in range(GR):
                    pe.wait_ge(s["x1_ready"], g.n * GR + k + 1)
                    for c in range(DC):
                        mm = nc.tensor.matmul(ps_zt[:, c, k * N:(k + 1) * N], x1[:, g.par, k, c * P:(c + 1) * P],
                                              gp[:, g.par, k, :], start=True, stop=True)
                mm.then_inc(s["z_done"], 1)

            def w1_product(g):
                for hc in range(HC):
                    if hc == 2:
                        wait(pe, s["f_ready"], g.n * GR - GR)
                    for c in range(DC):
                        if hc == 0:
                            pe.wait_ge(s["zt_lo_ready"], g.n * DC + c + 1)
                        mm = split_product(ps[:, W1_BANK[hc], :],
                                           (w1_hi[:, c, hc * P:(hc + 1) * P], w1_lo[:, c, hc * P:(hc + 1) * P]),
                                           (zt_hi[:, c, :], zt_lo[:, c, :]), c == 0, c == DC - 1)
                    mm.then_inc(s["w1_done"], 1)

            def w2_product(g, n, k):
                if k == 2:
                    pe.wait_ge(s["u0_ready"], g.n * GR + 1)
                if k == 3:
                    pe.wait_ge(s["pcol_ready"], n.n + 1)
                for hc in range(HC):
                    if k == 0:
                        pe.wait_ge(s["h_lo_ready" if hc else "h_lo0_ready"], g.n * (HC - 1) + hc if hc else g.n + 1)
                    if k == 0 and hc == HC - 1:
                        pe.wait_ge(s["h_ready"], g.n * HC + HC)
                    mm = split_product(ps[:, W2_BANK[k], 0:W2N],
                                       (h_hi[:, hc, k * N:(k + 1) * N], h_lo[:, hc, k * N:(k + 1) * N]),
                                       (w2_hi[:, hc, :], w2_lo[:, hc, :]), hc == 0, hc == HC - 1)
                mm.then_inc(s["w2_done"], 1)

            def q_transposes(g, q_t):
                pe.wait_ge(s["q_ready"], g.n + 1)
                for k in range(GR):
                    mm = nc.tensor.transpose(q_t[:, k, :], q[:, k * N:(k + 1) * N], ident[:])
                mm.then_inc(s["qt_done"], 1)

            def w2_last(g):
                for hc in range(HC):
                    if hc == HC - 1:
                        q_transposes(g, ps_last_qt)
                    pe.wait_ge(s["h_lo_ready" if hc else "h_lo0_ready"], g.n * (HC - 1) + hc if hc else g.n + 1)
                    if hc == 0:
                        pe.wait_ge(s["gp_ready"], g.n + 1)
                        pe.wait_ge(s["ssq_ready"], g.n)
                        pe.wait_ge(s["u0_ready"], g.n * GR)
                        pe.wait_ge(s["h_ready"], g.n * HC + 2)
                    for k in range(GR):
                        mm = split_product(ps[:, LAST_BANK[k], 0:W2N],
                                           (h_hi[:, hc, k * N:(k + 1) * N], h_lo[:, hc, k * N:(k + 1) * N]),
                                           (w2_hi[:, hc, :], w2_lo[:, hc, :]), hc == 0, hc == HC - 1)
                        if hc == HC - 1:
                            mm.then_inc(s["w2_done"], 1)

            def c2_product(g, h_group):
                pe.wait_ge(s["h_ready"], h_group.n * HC + HC)
                pe.wait_ge(s["gp_lo_ready"], g.n + 1)
                pe.wait_ge(s["u_lo_ready"], g.n + 1)
                for k in range(GR):
                    mm = split_product(ps_c2[:, k, :], (gp_hi[:, g.par, k, :], gp_lo[:, g.par, k, :]),
                                       (u_hi[:, k, :], u_lo[:, k, :]), True, True)
                mm.then_inc(s["c2_done"], GR)

            def c2_last(g, ks, o):
                for k in ks:
                    pe.wait_ge(s["u_ready"], g.n * GR + k + 1)
                    mm = nc.tensor.matmul(o[:, k, :], gp[:, g.par, k, :], u[:, k, :], start=True, stop=True)
                mm.then_inc(s["c2_done"], len(ks))

            def step(g, n, m, last):
                z_product(g)
                t_product(n)
                transpose_incidence(n)
                w1_product(g)
                s_product(n)
                v_product(n, (0, 1))
                w_transpose(n)
                v_product(n, (2, 3))
                g_product(n)
                if last:
                    c2_product(last, g)
                else:
                    pe.wait_ge(s["w2_lo_ready"], 1)
                p_transpose(n)
                w2_product(g, n, 0)
                w2_product(g, n, 1)
                w2_product(g, n, 2)
                if m:
                    transpose_inputs(m)
                pe.wait_ge(s["gp_ready"], n.n + 1)
                q_transposes(g, ps_qt)
                w2_product(g, n, 3)

            first = Group(0, 0)
            warm_up()
            transpose_inputs(first)
            wqk_transposes()
            pe.wait_ge(s["ones_ready"], 1)
            transpose_incidence(first)
            m_product()
            w1_transposes()
            pe.wait_ge(s["m_lo_ready"], 1)
            t_product(first)
            w2_transposes()
            s_product(first)
            g_product(first)
            pe.wait_ge(s["wv_lo_ready"], 1)
            v_product(first, (0,))
            w_transpose(first)
            v_product(first, (1, 2, 3))
            p_transpose(first)
            w2_mean()
            transpose_inputs(Group(0, 1))
            w2_beta()
            pe.wait_ge(s["cbeta_ready"], 1)
            pe.wait_ge(s["w2c_ready"], 1)
            step(Group(0, 0), Group(0, 1), Group(0, 2), None)
            step(Group(0, 1), Group(0, 2), Group(0, 3), Group(0, 0))
            with pe.Fori(1, NG // 2 - 1) as it:
                for k in range(2):
                    step(Group(it, k), Group(it, k + 1), Group(it, k + 2), Group(it - 1, k + 1))
            step(Group(0, NG - 2), Group(0, NG - 1), None, Group(0, NG - 3))
            end = Group(0, NG - 1)
            z_product(end)
            w1_product(end)
            c2_last(Group(0, NG - 2), ALL, ps_v)
            w2_last(end)
            pe.wait_ge(s["ssq_ready"], NG)
            pe.wait_ge(s["h_ready"], NG * HC)
            for ks in HALVES:
                c2_last(end, ks, ps_c2)

        @block.scalar
        def _(act):
            def zt_high(g):
                act.wait_ge(s["z_done"], g.n + 1)
                for c in range(DC):
                    nc.scalar.copy(zt_hi[:, c, :], ps_zt[:, c, :]).then_inc(s["zt_hi_ready"], 1)

            def t_copy(n):
                act.wait_ge(s["t_done"], n.n + 1)
                nc.scalar.copy(tt[:], ps_xt).then_inc(s["tt_ready"], 1)

            def hidden(g, by_block=False, between=None):
                for hc in range(HC):
                    act.wait_ge(s["w1_done"], g.n * HC + hc + 1)
                    if hc == 0:
                        wait(act, s["h_lo0_ready"], g.n)
                    if hc == 1:
                        wait(act, s["h_lo_ready"], g.n * (HC - 1))
                    nc.scalar.activation(h[:, hc, :], ps[:, W1_BANK[hc], :], ACT.Relu,
                                         bias=vec_cols[:, hc:hc + 1]).then_inc(s["h_ready"], 1)
                    act.wait_ge(s["h_ready"], g.n * HC + hc + 1)
                    nc.scalar.copy(h_hi[:, hc, :], h[:, hc, :]).then_inc(s["h_hi_ready"], 1)
                if between:
                    softmax_exp(between)
                wait(act, s["q1_ready"], g.n)
                if by_block:
                    for hc in range(HC):
                        nc.scalar.activation(sq[:, hc, :], h[:, hc, :], ACT.Square).then_inc(s["sq_ready"], 1)
                else:
                    nc.scalar.activation(sq[:], h[:], ACT.Square).then_inc(s["sq_ready"], HC)

            def final_norm(g, ks=ALL):
                act.wait_ge(s["nmr_ready"], g.n * GR + ks[-1] + 1)
                if ks[0] == 0:
                    wait(act, stored[g.par], 16 * g.half)
                for k in ks:
                    nc.scalar.activation(y[:, g.par, k, :], f[:, g.par, k, :], ACT.Identity, bias=nmr[:, k:k + 1],
                                         scale=rstd2[:, k:k + 1]).then_inc(s["y_ready"], 1)

            def softmax_exp(n):
                act.wait_ge(s["wbias_ready"], n.n + 1)
                nc.scalar.activation(e_row[:], w_row[:], ACT.Exp, bias=w_bias[:], scale=1.0 / 16.0,
                                     accum_out=e_sum[:]).then_inc(s["e_ready"], 1)

            def u_copy(g, ks=ALL, bank=W2_BANK):
                for k in ks:
                    act.wait_ge(s["w2_done"], g.n * GR + k + 1)
                    if k == 0:
                        wait(act, s["u_ready"], g.n * GR)
                    nc.scalar.copy(u0[:, k, :], ps[:, bank[k], 0:W2N]).then_inc(s["u0_ready"], 1)

            def ht_copy(n):
                act.wait_ge(s["ht_done"], n.n + 1)
                wait(act, s["g_done"], n.n)
                nc.scalar.copy(ht[:], ps_ht).then_inc(s["ht_ready"], 1)

            def u_high(g):
                act.wait_ge(s["u_ready"], g.n * GR + GR)
                wait(act, s["c2_done"], g.n * GR)
                nc.scalar.copy(u_hi[:], u[:]).then_inc(s["u_hi_ready"], 1)

            def g_high(n):
                act.wait_ge(s["gp_ready"], n.n + 1)
                nc.scalar.copy(gp_hi[:, n.par], gp[:, n.par]).then_inc(s["gp_hi_ready"], 1)

            def xt_copy(m, parts=("xt", "high")):
                if "xt" in parts:
                    for c in range(DC):
                        act.wait_ge(s["xt_done"], m.n * DC + c + 1)
                        nc.scalar.copy(xt[:, c, :], ps_xt[:, c, :]).then_inc(s["xt_ready"], 1)
                if "high" in parts:
                    for c in range(DC):
                        act.wait_ge(s["xt_ready"], m.n * DC + c + 1)
                        nc.scalar.copy(xt_hi[:, c, :], xt[:, c, :]).then_inc(s["xt_hi_ready"], 1)

            def step(g, n, m, last, old):
                zt_high(g)
                t_copy(n)
                ht_copy(n)
                if last:
                    u_high(last)
                hidden(g, between=n)
                u_copy(g, (0,))
                g_high(n)
                u_copy(g, (1, 2))
                if m:
                    xt_copy(m)
                u_copy(g, (3,))
                if old and m:
                    final_norm(old)

            def w2_scaled():
                act.wait_ge(s["w2_tr"], 1)
                nc.scalar.copy(w2_t, ps[:, 6:8, :].rearrange("p a (b d) -> p (a b) d", d=D)).then_inc(
                    s["w2t_ready"], 1)
                act.wait_ge(s["vec_ready"], 1)
                for hc in range(HC):
                    off = (hc % 2) * D
                    ins = nc.scalar.activation(w2_g[:, hc, :], ps[:, 6 + hc // 2, off:off + D], ACT.Copy,
                                               scale=vec_cols[:, HC + hc:HC + hc + 1])
                ins.then_inc(s["w2g_ready"], 1)

            act.dma_start(wqk_raw[:], Wqk.rearrange("(c p) a -> p c a", p=P)).then_inc(s["wqk_loaded"], 16)
            act.dma_start(wv_raw[:], Wv.rearrange("(c p) a -> p c a", p=P)).then_inc(s["wv_loaded"], 16)
            first = Group(0, 0)
            xt_copy(first, ("xt",))
            act.wait_ge(s["wqk_tr"], 1)
            nc.scalar.copy(wq_t, ps[:, 4, :].rearrange("p (a d) -> p a d", a=DC)).then_inc(s["wqk_copied"], 1)
            ht_copy(first)
            xt_copy(first, ("high",))
            act.wait_ge(s["m_done"], 1)
            nc.scalar.copy(m_hi[:], ps[:, 6, :].rearrange("p (a d) -> p a d", a=DC)).then_inc(s["m_hi_ready"], 1)
            act.wait_ge(s["wv_loaded"], 16)
            nc.scalar.copy(wv_hi[:], wv_raw[:]).then_inc(s["wv_hi_ready"], 1)
            act.wait_ge(s["w1_tr"], 1)
            nc.scalar.copy(w1_hi[:], ps[:, 4:6, :]).then_inc(s["w1_hi_ready"], 1)
            t_copy(first)
            w2_scaled()
            softmax_exp(first)
            g_high(first)
            xt_copy(Group(0, 1))
            act.wait_ge(s["w2beta_done"], 1)
            nc.scalar.copy(cbeta[:], ps[:, 5, 0:D]).then_inc(s["cbeta_ready"], 1)
            act.wait_ge(s["consts_ready"], 1)
            act.wait_ge(s["w2c_ready"], 1)
            nc.scalar.copy(w2_hi[:, :, 0:D], w2_c[:]).then_inc(s["w2_hi_ready"], 1)
            step(Group(0, 0), Group(0, 1), Group(0, 2), None, None)
            step(Group(0, 1), Group(0, 2), Group(0, 3), Group(0, 0), None)
            with act.Fori(1, NG // 2 - 1) as it:
                for k in range(2):
                    step(Group(it, k), Group(it, k + 1), Group(it, k + 2), Group(it - 1, k + 1), Group(it - 1, k))
            step(Group(0, NG - 2), Group(0, NG - 1), None, Group(0, NG - 3), Group(0, NG - 4))
            end = Group(0, NG - 1)
            zt_high(end)
            final_norm(Group(0, NG - 4))
            hidden(end, by_block=True)
            final_norm(Group(0, NG - 3))
            u_copy(end, ALL, LAST_BANK)
            final_norm(Group(0, NG - 2))
            final_norm(end, HALVES[0])

        @block.vector
        def _(dve):
            V = nc.vector

            def w1_low():
                dve.wait_ge(s["w1_hi_ready"], 1)
                V.tensor_tensor(w1_lo[:], ps[:, 4:6, :], w1_hi[:].bitcast(F32), ALU.subtract).then_inc(
                    s["w1_lo_ready"], 1)

            def w2_centred():
                dve.wait_ge(s["w2mean_done"], 1)
                dve.wait_ge(s["w2g_ready"], 1)
                V.tensor_tensor(w2_c[:], w2_g, ps[:, 4, 0:D].unsqueeze(1).to_broadcast([P, HC, D]),
                                ALU.subtract).then_inc(s["w2c_ready"], 1)

            def xt_low(m):
                for c in range(DC):
                    dve.wait_ge(s["xt_hi_ready"], m.n * DC + c + 1)
                    V.tensor_tensor(xt_lo[:, c, :], xt[:, c, :], xt_hi[:, c, :].bitcast(F32),
                                    ALU.subtract).then_inc(s["xt_lo_ready"], 1)

            def final_sum(g, ks=ALL, c2=ps_c2, read=None):
                part = slice(ks[0], ks[-1] + 1)
                done = g.n * GR + ks[-1] + 1
                dve.wait_ge(s["c2_done"], done)
                dve.wait_ge(s["base_ready"], g.n + 1)
                if ks[0] == 0:
                    wait(dve, s["y_ready"], (read.n * GR + GR) if read else g.n * GR)
                V.tensor_tensor(f[:, g.par, part], c2[:, part], base[:, part], ALU.add).then_inc(s["f_ready"], len(ks))

            def final_stats(g, ks=ALL):
                dve.wait_ge(s["f_ready"], g.n * GR + ks[-1] + 1)
                for k in ks:
                    ins = V.bn_stats(st2[:, k, :], f[:, g.par, k, :])
                ins.then_inc(s["st2_ready"], len(ks))

            def final_aggregate(g, ks=ALL):
                part = slice(ks[0], ks[-1] + 1)
                done = g.n * GR + ks[-1] + 1
                plain(dve, s["vec_ready"])
                dve.wait_ge(s["st2_ready"], done)
                for k in ks:
                    ins = V.bn_aggr(mv2[:, k, :], st2[:, k, :])
                ins.then_inc(s["mv2_ready"], len(ks))
                dve.wait_ge(s["mv2_ready"], done)
                V.tensor_scalar(ve2[:, part], mv2[:, part, 1], EPS, None, ALU.add).then_inc(s["ve2_ready"], len(ks))

            def final_bias(g, ks=ALL):
                part = slice(ks[0], ks[-1] + 1)
                dve.wait_ge(s["rstd2_ready"], g.n * GR + ks[-1] + 1)
                V.scalar_tensor_tensor(out=nmr[:, part], in0=mv2[:, part, 0], scalar=-1.0, in1=rstd2[:, part],
                                       op0=ALU.mult, op1=ALU.mult).then_inc(s["nmr_ready"], len(ks))

            def final_norm_last(g, ks):
                dve.wait_ge(s["rstd2_ready"], g.n * GR + ks[-1] + 1)
                dve.wait_ge(stored[g.par], 16 * g.half)
                for k in ks:
                    V.tensor_scalar(y[:, g.par, k, :], f[:, g.par, k, :], mv2[:, k, 0:1], rstd2[:, k:k + 1],
                                    ALU.subtract, ALU.mult).then_inc(s["y2_ready"], 1)

            def zt_low(g):
                for c in range(DC):
                    dve.wait_ge(s["zt_hi_ready"], g.n * DC + c + 1)
                    V.tensor_tensor(zt_lo[:, c, :], ps_zt[:, c, :], zt_hi[:, c, :].bitcast(F32),
                                    ALU.subtract).then_inc(s["zt_lo_ready"], 1)

            def incidence(m):
                dve.wait_ge(a_loaded[m.par], 16 * (m.half + 1))
                wait(dve, s["he_ready"], m.n)
                wait(dve, s["ht_done"], m.n)
                V.tensor_scalar(hn[:], a_in[:, m.par], 0.0, None, ALU.not_equal).then_inc(s["hn_ready"], 1)

            def sizes_and_degrees(n):
                dve.wait_ge(s["ht_ready"], n.n + 1)
                V.tensor_reduce(cnt[:], ht[:], AX_X, ALU.add).then_inc(s["cnt_ready"], 1)
                dve.wait_ge(s["he_ready"], n.n + 1)
                V.tensor_reduce(deg[:], he[:], AX_X, ALU.add).then_inc(s["deg_ready"], 1)
                dve.wait_ge(s["cnt_ready"], n.n + 1)
                V.tensor_scalar(cnt1[:], cnt[:], 1.0, None, ALU.max).then_inc(s["cnt1_ready"], 1)
                dve.wait_ge(s["deg_ready"], n.n + 1)
                V.scalar_tensor_tensor(out=deg1[:], in0=deg[:], scalar=0.0, in1=deg[:], op0=ALU.is_le,
                                       op1=ALU.max).then_inc(s["deg1_ready"], 1)
                dve.wait_ge(s["cnt1_ready"], n.n + 1)
                wait(dve, s["rr_ready"], n.n)
                V.reciprocal(be[:], cnt1[:]).then_inc(s["be_ready"], 1)
                dve.wait_ge(s["deg1_ready"], n.n + 1)
                V.reciprocal(deg_inv[:], deg1[:]).then_inc(s["dinv_ready"], 1)
                dve.wait_ge(s["dinv_ready"], n.n + 1)
                wait(dve, s["dn_stored"], 16 * n.n)
                V.scalar_tensor_tensor(out=dn[:], in0=deg[:], scalar=0.0, in1=deg_inv[:], op0=ALU.is_gt,
                                       op1=ALU.mult).then_inc(s["dn_ready"], 1)

            def hidden_low(g, hc):
                dve.wait_ge(s["h_hi_ready"], g.n * HC + hc + 1)
                V.tensor_tensor(h_lo[:, hc, :], h[:, hc, :], h_hi[:, hc, :].bitcast(F32),
                                ALU.subtract).then_inc(s["h_lo_ready"], 1)

            def dots(n):
                dve.wait_ge(s["am_ready"], n.n + 1)
                dve.wait_ge(s["s_done"], n.n + 1)
                for k in range(GR):
                    V.tensor_tensor_reduce(dot_junk[:, k, :], ps_s[:, k, :], am[:, k, :], 1.0, 0.0, ALU.mult, ALU.add,
                                           w_col[:, k:k + 1]).then_inc(s["w_ready"], 1)

            def g_scale(n):
                dve.wait_ge(s["g_done"], n.n + 1)
                dve.wait_ge(s["dn_rows_loaded"], 16 * (n.n + 1))
                wait(dve, s["c2_done"], n.n * GR - GR)
                V.tensor_tensor(gp[:, n.par], ps_g, dn_rows[:].rearrange("p n g -> p g n"), ALU.mult).then_inc(
                    s["gp_ready"], 1)

            def softmax_max(n):
                dve.wait_ge(s["wt_done"], n.n + 1)
                V.tensor_tensor(w_row[:], ps[0:GR, 2, 0:N], mrow_in[:, n.par], ALU.mult).then_inc(s["wrow_ready"], 1)
                dve.wait_ge(s["wrow_ready"], n.n + 1)
                V.tensor_reduce(w_max[:], w_row[:], AX_X, ALU.max).then_inc(s["wmax_ready"], 1)
                dve.wait_ge(s["wmax_ready"], n.n + 1)
                V.tensor_scalar(w_bias[:], w_max[:], -1.0 / 16.0, None, ALU.mult).then_inc(s["wbias_ready"], 1)

            def softmax_scale(n):
                dve.wait_ge(s["e_ready"], n.n + 1)
                V.reciprocal(e_inv[:], e_sum[:]).then_inc(s["einv_ready"], 1)
                dve.wait_ge(s["einv_ready"], n.n + 1)
                V.tensor_scalar(p_row[:], e_row[:], e_inv[:], None, ALU.mult).then_inc(s["prow_ready"], 1)

            def residual(n):
                dve.wait_ge(s["pcol_done"], n.n + 1)
                V.tensor_copy(p_col[:], ps[:, 2, N:N + GR]).then_inc(s["pcol_ready"], 1)
                dve.wait_ge(s["pcol_ready"], n.n + 1)
                for k in range(GR):
                    dve.wait_ge(s["v_done"], n.n * GR + k + 1)
                    V.scalar_tensor_tensor(out=r1[:, k, :], in0=ps_v[:, k, :], scalar=p_col[:, k:k + 1],
                                           in1=x_in[:, n.par, k, :], op0=ALU.mult,
                                           op1=ALU.add).then_inc(s["r1_ready"], 1)

            def x1_stats(n):
                for k in range(GR):
                    dve.wait_ge(s["r1_ready"], n.n * GR + k + 1)
                    V.bn_stats(st1[:, k, :], r1[:, k, :]).then_inc(s["st1_ready"], 1)

            def x1_aggregate(n):
                plain(dve, s["vec_ready"])
                dve.wait_ge(s["st1_ready"], n.n * GR + GR)
                for k in range(GR):
                    ins = V.bn_aggr(mv1[:, k, :], st1[:, k, :])
                ins.then_inc(s["mv1_ready"], 1)
                dve.wait_ge(s["mv1_ready"], n.n + 1)
                V.tensor_scalar(ve1[:], mv1[:, :, 1], EPS, None, ALU.add).then_inc(s["ve1_ready"], 1)

            def x1_apply(n):
                dve.wait_ge(s["rstd1_ready"], n.n + 1)
                wait(dve, s["base_ready"], n.n - 1)
                for k in range(GR):
                    V.tensor_scalar(x1[:, n.par, k, :], r1[:, k, :], mv1[:, k, 0:1], rstd1[:, k:k + 1],
                                    ALU.subtract, ALU.mult).then_inc(s["x1_ready"], 1)

            def square_sums(g, q_t):
                dve.wait_ge(s["qt_done"], g.n + 1)
                V.tensor_reduce(ssq[:], q_t, AX_X, ALU.add).then_inc(s["ssq_ready"], 1)

            def square_blocks(g, half):
                dve.wait_ge(s["sq_ready"], g.n * HC + 2 * half + 2)
                V.tensor_tensor(q1[:, half, :], sq[:, 2 * half, :], sq[:, 2 * half + 1, :], ALU.add).then_inc(
                    s["q1_ready"], 1)
                if half == 1:
                    dve.wait_ge(s["q1_ready"], g.n + 2)
                    V.tensor_tensor(q[:], q1[:, 0, :], q1[:, 1, :], ALU.add).then_inc(s["q_ready"], 1)

            def hidden_stats(g, ks=ALL):
                part = slice(ks[0], ks[-1] + 1)
                done = g.n * GR + ks[-1] + 1
                dve.wait_ge(s["u0_ready"], done)
                V.scalar_tensor_tensor(out=hmu2[:, part], in0=u0[:, part, D], scalar=-1.0, in1=u0[:, part, D],
                                       op0=ALU.mult, op1=ALU.mult).then_inc(s["hmu2_ready"], len(ks))
                dve.wait_ge(s["hmu2_ready"], done)
                V.scalar_tensor_tensor(out=hvar[:, part], in0=ssq[:, part], scalar=1.0 / DH, in1=hmu2[:, part],
                                       op0=ALU.mult, op1=ALU.add).then_inc(s["hvar_ready"], len(ks))
                dve.wait_ge(s["hvar_ready"], done)
                V.tensor_scalar(hve[:, part], hvar[:, part], 0.0, EPS, ALU.max, ALU.add).then_inc(
                    s["hve_ready"], len(ks))

            def u_rows(g, ks=ALL, before=None):
                dve.wait_ge(s["rs_ready"], g.n * GR + ks[-1] + 1)
                if before:
                    dve.wait_ge(s["c2_done"], before.n * GR + GR)
                elif ks[0] == 0:
                    wait(dve, s["u_lo_ready"], g.n)
                for k in ks:
                    V.scalar_tensor_tensor(out=u[:, k, :], in0=u0[:, k, 0:D], scalar=rs[:, k:k + 1], in1=cbeta[:],
                                           op0=ALU.mult, op1=ALU.add).then_inc(s["u_ready"], 1)

            def step(g, n, m, last, old):
                zt_low(g)
                if old:
                    final_sum(old)
                if last:
                    u_rows(last)
                sizes_and_degrees(n)
                if old:
                    final_stats(old)
                dots(n)
                hidden_low(g, 1)
                softmax_max(n)
                hidden_low(g, 2)
                hidden_low(g, 3)
                softmax_scale(n)
                if old:
                    final_aggregate(old)
                g_scale(n)
                if m:
                    incidence(m)
                residual(n)
                x1_stats(n)
                x1_aggregate(n)
                if old:
                    final_bias(old)
                x1_apply(n)
                if m:
                    xt_low(m)
                square_sums(g, ps_qt)
                hidden_stats(g)

            first = Group(0, 0)
            dve.wait_ge(s["wqk_tr"], 2)
            V.tensor_copy(wk_t, ps[:, 5, :].rearrange("p (a d) -> p a d", a=DC)).then_inc(s["wqk_copied"], 1)
            incidence(first)
            xt_low(first)
            dve.wait_ge(s["m_hi_ready"], 1)
            V.tensor_tensor(m_lo[:], ps[:, 6, :].rearrange("p (a d) -> p a d", a=DC), m_hi[:].bitcast(F32),
                            ALU.subtract).then_inc(s["m_lo_ready"], 1)
            sizes_and_degrees(first)
            dve.wait_ge(s["vec_tr"], 1)
            V.tensor_copy(vec_cols[:], ps[:, 7, 0:3 * HC]).then_inc(s["vec_ready"], 1)
            w1_low()
            dots(first)
            softmax_max(first)
            softmax_scale(first)
            g_scale(first)
            residual(first)
            x1_stats(first)
            x1_aggregate(first)
            w2_centred()
            x1_apply(first)
            incidence(Group(0, 1))
            xt_low(Group(0, 1))
            dve.wait_ge(s["cbeta_ready"], 1)
            step(Group(0, 0), Group(0, 1), Group(0, 2), None, None)
            step(Group(0, 1), Group(0, 2), Group(0, 3), Group(0, 0), None)
            with dve.Fori(1, NG // 2 - 1) as it:
                for k in range(2):
                    step(Group(it, k), Group(it, k + 1), Group(it, k + 2), Group(it - 1, k + 1), Group(it - 1, k))
            step(Group(0, NG - 2), Group(0, NG - 1), None, Group(0, NG - 3), Group(0, NG - 4))
            end = Group(0, NG - 1)
            zt_low(end)
            final_sum(Group(0, NG - 3), read=Group(0, NG - 5))
            u_rows(Group(0, NG - 2))
            final_stats(Group(0, NG - 3))
            final_aggregate(Group(0, NG - 3))
            for hc in range(1, HC):
                hidden_low(end, hc)
            final_sum(Group(0, NG - 2), ALL, ps_v, Group(0, NG - 4))
            final_bias(Group(0, NG - 3))
            square_blocks(end, 0)
            square_blocks(end, 1)
            final_stats(Group(0, NG - 2))
            square_sums(end, ps_last_qt)
            for ks in HALVES:
                hidden_stats(end, ks)
            final_aggregate(Group(0, NG - 2))
            for ks in HALVES:
                u_rows(end, ks, Group(0, NG - 2))
            final_bias(Group(0, NG - 2))
            for ks in HALVES:
                final_sum(end, ks, read=Group(0, NG - 3))
                final_stats(end, ks)
                final_aggregate(end, ks)
            final_bias(end, HALVES[0])
            final_norm_last(end, HALVES[1])

        @block.gpsimd
        def _(pool):
            Q = nc.gpsimd

            def setup():
                Q.memset(ident[:], 0.0).then_inc(s["ident_zero"], 1)
                pool.wait_ge(s["ident_zero"], 1)
                Q.affine_select(out=ident[:], in_=ident[:], compare_op=ALU.not_equal, fill=1.0, base=0,
                                pattern=[[-1, P]], channel_multiplier=1).then_inc(s["ident_ready"], 1)
                pool.wait_ge(s["ident_ready"], 1)
                Q.memset(ones[:], 1.0)
                Q.memset(neg_half[:], -0.5)
                Q.tensor_copy(ident_bf[:], ident[:]).then_inc(s["ones_ready"], 1)
                Q.memset(w2_hi[:, :, D:W2N].bitcast(F32), 1.0 / DH)
                Q.memset(w2_lo[:, :, D:W2N].bitcast(F32), 0.0)
                Q.memset(ones_mean[:], 1.0 / DH).then_inc(s["consts_ready"], 1)

            def weight_parts():
                pool.wait_ge(s["wv_hi_ready"], 1)
                Q.tensor_tensor(wv_lo[:], wv_raw[:], wv_hi[:].bitcast(F32), ALU.subtract).then_inc(s["wv_lo_ready"], 1)
                pool.wait_ge(s["vec_ready"], 1)
                Q.tensor_tensor(beta_rows, vec_cols[:, 2 * HC:3 * HC].unsqueeze(2).to_broadcast([P, HC, P]),
                                ones[:].unsqueeze(1).to_broadcast([P, HC, P]), ALU.mult).then_inc(s["beta_ready"], 1)

            def w2_low():
                pool.wait_ge(s["w2_hi_ready"], 1)
                Q.tensor_tensor(w2_lo[:, :, 0:D], w2_c[:], w2_hi[:, :, 0:D].bitcast(F32),
                                ALU.subtract).then_inc(s["w2_lo_ready"], 1)

            def masked_adj(n):
                pool.wait_ge(m_loaded[n.par], 16 * M_LOADS * (n.half + 1))
                wait(pool, s["w_ready"], n.n * GR)
                Q.tensor_tensor(am[:], a_in[:, n.par], mask_in[:, n.par], ALU.mult).then_inc(s["am_ready"], 1)

            def base_rows_0(g):
                pool.wait_ge(s["x1_ready"], g.n * GR + GR)
                wait(pool, s["base_ready"], g.n)
                Q.tensor_tensor(base0[:], x1[:, g.par], b2_rows[:].unsqueeze(1).to_broadcast([P, GR, D]),
                                ALU.add).then_inc(s["base0_ready"], 1)

            def base_rows(g):
                pool.wait_ge(s["base0_ready"], g.n + 1)
                wait(pool, s["f_ready"], g.n * GR)
                Q.tensor_tensor(base[:], base0[:], x1[:, g.par], ALU.add).then_inc(s["base_ready"], 1)

            def final_rstd(g, ks=ALL):
                part = slice(ks[0], ks[-1] + 1)
                pool.wait_ge(s["ve2_ready"], g.n * GR + ks[-1] + 1)
                if ks[0] == 0:
                    wait(pool, s["y_ready"], g.n * GR)
                Q.tensor_tensor(rstd2[:, part], ve2[:, part], neg_half[:, part], ALU.pow).then_inc(
                    s["rstd2_ready"], len(ks))

            def edge_weights(n):
                pool.wait_ge(m_loaded[n.par], 16 * M_LOADS * (n.half + 1))
                pool.wait_ge(s["hn_ready"], n.n + 1)
                wait(pool, s["deg_ready"], n.n)
                Q.tensor_tensor(he[:], hn[:], edge_in[:, n.par], ALU.mult).then_inc(s["he_ready"], 1)

            def r_scale(n):
                pool.wait_ge(s["be_ready"], n.n + 1)
                wait(pool, s["g_done"], n.n)
                Q.tensor_tensor(rr[:], ht[:], be[:].unsqueeze(2).to_broadcast([P, GR, N]), ALU.mult).then_inc(
                    s["rr_ready"], 1)

            def square_blocks(g):
                pool.wait_ge(s["sq_ready"], g.n * HC + HC)
                Q.tensor_tensor(q1[:], sq[:, 0:2, :], sq[:, 2:4, :], ALU.add).then_inc(s["q1_ready"], 1)
                pool.wait_ge(s["q1_ready"], g.n + 1)
                wait(pool, s["qt_done"], g.n)
                Q.tensor_tensor(q[:], q1[:, 0, :], q1[:, 1, :], ALU.add).then_inc(s["q_ready"], 1)

            def hidden_low_0(g):
                pool.wait_ge(s["h_hi_ready"], g.n * HC + 1)
                Q.tensor_tensor(h_lo[:, 0, :], h[:, 0, :], h_hi[:, 0, :].bitcast(F32),
                                ALU.subtract).then_inc(s["h_lo0_ready"], 1)

            def u_low(g):
                pool.wait_ge(s["u_hi_ready"], g.n + 1)
                Q.tensor_tensor(u_lo[:], u[:], u_hi[:].bitcast(F32), ALU.subtract).then_inc(s["u_lo_ready"], 1)

            def g_low(n):
                pool.wait_ge(s["gp_hi_ready"], n.n + 1)
                Q.tensor_tensor(gp_lo[:, n.par], gp[:, n.par], gp_hi[:, n.par].bitcast(F32),
                                ALU.subtract).then_inc(s["gp_lo_ready"], 1)

            def hidden_rstd(g, ks=ALL):
                part = slice(ks[0], ks[-1] + 1)
                pool.wait_ge(s["hve_ready"], g.n * GR + ks[-1] + 1)
                if ks[0] == 0:
                    wait(pool, s["u_ready"], g.n * GR)
                Q.tensor_tensor(rs[:, part], hve[:, part], neg_half[:, part], ALU.pow).then_inc(
                    s["rs_ready"], len(ks))

            def x1_rstd(n):
                pool.wait_ge(s["ve1_ready"], n.n + 1)
                Q.tensor_tensor(rstd1[:], ve1[:], neg_half[:], ALU.pow).then_inc(s["rstd1_ready"], 1)

            def step(g, n, last, old):
                edge_weights(n)
                masked_adj(n)
                if last:
                    base_rows(last)
                    u_low(last)
                r_scale(n)
                hidden_low_0(g)
                if old:
                    final_rstd(old)
                square_blocks(g)
                x1_rstd(n)
                g_low(n)
                base_rows_0(g)
                hidden_rstd(g)

            setup()
            first = Group(0, 0)
            edge_weights(first)
            masked_adj(first)
            r_scale(first)
            weight_parts()
            x1_rstd(first)
            g_low(first)
            w2_low()
            pool.wait_ge(s["b2_loaded"], 16)
            step(Group(0, 0), Group(0, 1), None, None)
            step(Group(0, 1), Group(0, 2), Group(0, 0), None)
            with pool.Fori(1, NG // 2 - 1) as it:
                for k in range(2):
                    step(Group(it, k), Group(it, k + 1), Group(it - 1, k + 1), Group(it - 1, k))
            step(Group(0, NG - 2), Group(0, NG - 1), Group(0, NG - 3), Group(0, NG - 4))
            end = Group(0, NG - 1)
            base_rows(Group(0, NG - 2))
            hidden_low_0(end)
            final_rstd(Group(0, NG - 3))
            base_rows_0(end)
            base_rows(end)
            for ks in HALVES:
                hidden_rstd(end, ks)
            final_rstd(Group(0, NG - 2))
            for ks in HALVES:
                final_rstd(end, ks)


_INS = ['x', 'adj', 'nodemask', 'L0_gnn_Wqk', 'L0_gnn_Wv', 'L1_gnn_W1', 'L1_gnn_b1', 'L1_gnn_gamma', 'L1_gnn_beta',
        'L1_gnn_W2', 'L1_gnn_b2']


def kernel(**inputs):
    import numpy as _np
    import concourse.bacc as _bacc
    from concourse import mybir as _mybir
    from concourse.bass_utils import run_bass_kernel_spmd as _run

    nc = _bacc.Bacc("TRN2", target_bir_lowering=False, num_devices=1)
    arrays, args = {}, []
    for name in _INS:
        a = _np.ascontiguousarray(inputs[name])
        arrays[f"in_{name}"] = a
        args.append(nc.dram_tensor(f"in_{name}", a.shape, _mybir.dt.from_np(a.dtype), kind="ExternalInput").ap())
    shape = inputs['x'].shape
    args.append(nc.dram_tensor("out_x", shape, _mybir.dt.float32, kind="ExternalOutput").ap())
    build_program(nc, *args)
    r = _run(nc, [arrays], core_ids=[0])
    return r.results[0]["out_x"]
```
